# Optimizing a Trainium2 kernel written in Bass

```python
import numpy as np
import jax
import jax.numpy as jnp

def _softmax(x, axis=-1):
    return jax.nn.softmax(x, axis=axis)

def _gelu(x):
    return jax.nn.gelu(x, approximate=True)

def _silu(x):
    return jax.nn.silu(x)

def _sigmoid(x):
    return jax.nn.sigmoid(x)

def _layernorm(x, axis=-1, eps=1e-05):
    m = jnp.mean(x, axis=axis, keepdims=True)
    v = jnp.var(x, axis=axis, keepdims=True)
    return (x - m) / jnp.sqrt(v + eps)

def _scatter_add(tgt, idx, src, axis=0):
    return tgt.at[idx].add(src)

def _segment_sum(src, seg, n):
    return jax.ops.segment_sum(src, seg, n)
kernel_name = 'mk_adj_resnorm_d4_adj_r2_f6f165'

def setup_inputs(seed: int=0):
    np.random.seed(seed)
    _w = jnp.asarray

    def _rec_inputs():
        import jax
        import jax.numpy as jnp
        _gk = jax.random.key(seed)
        x = -0.000929 + 1 * jax.random.normal(jax.random.fold_in(_gk, 1), (4096, 128), jnp.float32)
        _w = (1.0 + jnp.arange(4096, dtype=jnp.float32)) ** (-0.5)
        _w = _w / _w.mean()
        _pij = jnp.clip(0.00195312 * _w[:, None] * _w[None, :], 0.0, 1.0)
        _a = jax.random.uniform(jax.random.fold_in(_gk, 2), (4096, 4096)) < _pij
        _a = jnp.logical_or(_a, jnp.swapaxes(_a, -1, -2))
        _a = jnp.logical_or(_a, jnp.eye(4096, dtype=bool))
        _af = _a.astype(jnp.float32)
        _af = _af * jax.random.uniform(jax.random.fold_in(_gk, 3), (4096, 4096), jnp.float32, 0.05, 0.0598829)
        adj = _af
        return (x, adj)
    x, adj = _rec_inputs()

    def _L0_gnn_setup():
        import jax, jax.numpy as jnp
        import numpy as np
        N, F_DIM, H_DIM = (4096, 128, 128)

        def _gwnn_layer(features, wavelets, wavelets_inv, W, filt):
            xw = features @ W
            spec = wavelets_inv @ xw
            spec = filt[:, None] * spec
            return wavelets @ spec
        key = jax.random.key(seed)
        ks = jax.random.split(key, 7)
        inp = {'input': jax.random.normal(ks[0], (N, F_DIM), dtype=jnp.float32), 'wavelets': jax.random.normal(ks[1], (N, N), dtype=jnp.float32) / np.sqrt(N), 'wavelets_inv': jax.random.normal(ks[2], (N, N), dtype=jnp.float32) / np.sqrt(N), 'W1': jax.random.uniform(ks[3], (F_DIM, H_DIM), dtype=jnp.float32, minval=-np.sqrt(6.0 / (F_DIM + H_DIM)), maxval=np.sqrt(6.0 / (F_DIM + H_DIM))), 'f1': jax.random.uniform(ks[4], (N,), dtype=jnp.float32, minval=0.9, maxval=1.1), 'W2': jax.random.uniform(ks[5], (H_DIM, H_DIM), dtype=jnp.float32, minval=-np.sqrt(6.0 / (H_DIM + H_DIM)), maxval=np.sqrt(6.0 / (H_DIM + H_DIM))), 'f2': jax.random.uniform(ks[6], (N,), dtype=jnp.float32, minval=0.9, maxval=1.1)}
        return inp
    _L0_gnn_all = _L0_gnn_setup()
    _L0_gnn_in = {k: v for k, v in _L0_gnn_all.items() if k in ('W1', 'f1', 'W2', 'f2')}
    del _L0_gnn_all

    def _L1_gnn_setup():
        import jax, jax.numpy as jnp
        import numpy as np
        N, D = (4096, 128)
        key = jax.random.key(seed)
        k1, k2, k3 = jax.random.split(key, 3)
        x = jax.random.normal(k1, (N, D), dtype=jnp.float32)
        adj = jax.random.randint(k2, (N, N), 0, 2).astype(jnp.float32)
        beta = jax.random.uniform(k3, (1,), dtype=jnp.float32)
        return {'x': x, 'adj': adj, 'beta': beta}
    _L1_gnn_all = _L1_gnn_setup()
    _L1_gnn_in = {k: v for k, v in _L1_gnn_all.items() if k in ('beta',)}
    del _L1_gnn_all

    def _L2_gnn_setup():
        import jax, jax.numpy as jnp
        import numpy as np
        N, DIM = (8192, 128)

        def _gru_cell(x, h, W_ih, W_hh, b_ih, b_hh):
            gi = x @ W_ih.T + b_ih
            gh = h @ W_hh.T + b_hh
            i_r, i_z, i_n = jnp.split(gi, 3, axis=-1)
            h_r, h_z, h_n = jnp.split(gh, 3, axis=-1)
            r = jax.nn.sigmoid(i_r + h_r)
            z = jax.nn.sigmoid(i_z + h_z)
            n = jnp.tanh(i_n + r * h_n)
            return (1.0 - z) * n + z * h
        key = jax.random.key(seed)
        ks = jax.random.split(key, 8)
        states = jax.random.normal(ks[0], (N, DIM), dtype=jnp.float32)
        adj = jax.random.uniform(ks[1], (N, N), dtype=jnp.float32)
        s = 1.0 / np.sqrt(DIM)
        W_msg = jax.random.uniform(ks[2], (DIM, DIM), minval=-s, maxval=s, dtype=jnp.float32)
        b_msg = jax.random.uniform(ks[3], (DIM,), minval=-s, maxval=s, dtype=jnp.float32)
        W_ih = jax.random.uniform(ks[4], (3 * DIM, DIM), minval=-s, maxval=s, dtype=jnp.float32)
        W_hh = jax.random.uniform(ks[5], (3 * DIM, DIM), minval=-s, maxval=s, dtype=jnp.float32)
        b_ih = jax.random.uniform(ks[6], (3 * DIM,), minval=-s, maxval=s, dtype=jnp.float32)
        b_hh = jax.random.uniform(ks[7], (3 * DIM,), minval=-s, maxval=s, dtype=jnp.float32)
        return {'states': states, 'adj': adj, 'W_msg': W_msg, 'b_msg': b_msg, 'W_ih': W_ih, 'W_hh': W_hh, 'b_ih': b_ih, 'b_hh': b_hh}
    _L2_gnn_all = _L2_gnn_setup()
    _L2_gnn_in = {k: v for k, v in _L2_gnn_all.items() if k in ('W_msg', 'b_msg', 'W_ih', 'W_hh', 'b_ih', 'b_hh')}
    del _L2_gnn_all

    def _L3_gnn_setup():
        import jax, jax.numpy as jnp
        import numpy as np
        key = jax.random.key(seed)
        k1, k2, k3, k4 = jax.random.split(key, 4)
        n, in_dim, out_dim = (8192, 128, 128)
        h = jax.random.normal(k1, (n, in_dim), dtype=jnp.float32)
        adj = jax.random.uniform(k2, (n, n), dtype=jnp.float32)
        W_self = jax.random.normal(k3, (in_dim, out_dim), dtype=jnp.float32) * (1.0 / np.sqrt(in_dim))
        W_neigh = jax.random.normal(k4, (in_dim, out_dim), dtype=jnp.float32) * (1.0 / np.sqrt(in_dim))
        return {'h': h, 'adj': adj, 'W_self': W_self, 'W_neigh': W_neigh}
    _L3_gnn_all = _L3_gnn_setup()
    _L3_gnn_in = {k: v for k, v in _L3_gnn_all.items() if k in ('W_self', 'W_neigh')}
    del _L3_gnn_all
    return {'x': x, 'adj': adj, 'L0_gnn_W1': _L0_gnn_in['W1'], 'L0_gnn_f1': _L0_gnn_in['f1'], 'L0_gnn_W2': _L0_gnn_in['W2'], 'L0_gnn_f2': _L0_gnn_in['f2'], 'L1_gnn_beta': _L1_gnn_in['beta'], 'L2_gnn_W_msg': _L2_gnn_in['W_msg'], 'L2_gnn_b_msg': _L2_gnn_in['b_msg'], 'L2_gnn_W_ih': _L2_gnn_in['W_ih'], 'L2_gnn_W_hh': _L2_gnn_in['W_hh'], 'L2_gnn_b_ih': _L2_gnn_in['b_ih'], 'L2_gnn_b_hh': _L2_gnn_in['b_hh'], 'L3_gnn_W_self': _L3_gnn_in['W_self'], 'L3_gnn_W_neigh': _L3_gnn_in['W_neigh']}

def reference(x, adj, L0_gnn_W1, L0_gnn_f1, L0_gnn_W2, L0_gnn_f2, L1_gnn_beta, L2_gnn_W_msg, L2_gnn_b_msg, L2_gnn_W_ih, L2_gnn_W_hh, L2_gnn_b_ih, L2_gnn_b_hh, L3_gnn_W_self, L3_gnn_W_neigh):
    import jax
    import jax.numpy as jnp

    def _L0_gnn_ref(input, wavelets, wavelets_inv, W1, f1, W2, f2):
        import jax, jax.numpy as jnp
        import numpy as np
        N, F_DIM, H_DIM = (4096, 128, 128)

        def _gwnn_layer(features, wavelets, wavelets_inv, W, filt):
            xw = features @ W
            spec = wavelets_inv @ xw
            spec = filt[:, None] * spec
            return wavelets @ spec
        h1 = jax.nn.relu(_gwnn_layer(input, wavelets, wavelets_inv, W1, f1))
        out = _gwnn_layer(h1, wavelets, wavelets_inv, W2, f2)
        return out

    def _L1_gnn_ref(x, adj, beta):
        import jax, jax.numpy as jnp
        import numpy as np
        N, D = (4096, 128)
        norm2 = jnp.linalg.norm(x, axis=1, keepdims=True)
        cos = beta * (x @ x.T) / (norm2 @ norm2.T + 1e-07)
        masked = cos + (1.0 - adj) * -1000000000.0
        P = jax.nn.softmax(masked, axis=1)
        return P @ x

    def _L2_gnn_ref(states, adj, W_msg, b_msg, W_ih, W_hh, b_ih, b_hh):
        import jax, jax.numpy as jnp
        import numpy as np
        N, DIM = (8192, 128)

        def _gru_cell(x, h, W_ih, W_hh, b_ih, b_hh):
            gi = x @ W_ih.T + b_ih
            gh = h @ W_hh.T + b_hh
            i_r, i_z, i_n = jnp.split(gi, 3, axis=-1)
            h_r, h_z, h_n = jnp.split(gh, 3, axis=-1)
            r = jax.nn.sigmoid(i_r + h_r)
            z = jax.nn.sigmoid(i_z + h_z)
            n = jnp.tanh(i_n + r * h_n)
            return (1.0 - z) * n + z * h
        agg = adj @ states
        msg = jax.nn.relu(agg @ W_msg.T + b_msg)
        return _gru_cell(msg, states, W_ih, W_hh, b_ih, b_hh)

    def _L3_gnn_ref(h, adj, W_self, W_neigh):
        import jax, jax.numpy as jnp
        import numpy as np
        deg = jnp.clip(jnp.sum(adj, axis=1, keepdims=True), 1.0)
        h_neigh = adj @ h / deg
        return h @ W_self + h_neigh @ W_neigh
    x = _layernorm(x + _L0_gnn_ref(x, adj, adj, L0_gnn_W1, L0_gnn_f1, L0_gnn_W2, L0_gnn_f2), axis=-1)
    x = _layernorm(x + _L1_gnn_ref(x, adj, L1_gnn_beta), axis=-1)
    x = _layernorm(x + _L2_gnn_ref(x, adj, L2_gnn_W_msg, L2_gnn_b_msg, L2_gnn_W_ih, L2_gnn_W_hh, L2_gnn_b_ih, L2_gnn_b_hh), axis=-1)
    x = _layernorm(x + _L3_gnn_ref(x, adj, L3_gnn_W_self, L3_gnn_W_neigh), axis=-1)
    return x

_drawn_inputs = setup_inputs


def setup_inputs(seed=0):
    import zlib

    import numpy as np

    out = dict(_drawn_inputs(seed))
    spreads = {}
    factors = {'L0_gnn_f1': 8.0,
     'L0_gnn_f2': 8.0,
     'L2_gnn_b_msg': 8.0,
     'L2_gnn_b_ih': 2.829,
     'L2_gnn_b_hh': 4.405}
    for name, (base, spread) in spreads.items():
        noise = np.random.default_rng([zlib.crc32(name.encode()), seed]).standard_normal(out[name].shape)
        drawn = base * np.exp(spread * noise) if base else spread * noise
        out[name] = jnp.asarray(drawn.astype(out[name].dtype))
    for name, factor in factors.items():
        out[name] = (out[name] * factor).astype(out[name].dtype)
    return out
```

```python
from contextlib import ExitStack

import concourse.bass as bass
from concourse import mybir

ALU = mybir.AluOpType
ACT = mybir.ActivationFunctionType
AX = mybir.AxisListType
F32 = mybir.dt.float32
F32R = mybir.dt.float32r
I32 = mybir.dt.int32
RMAX = bass.bass_isa.ReduceOp.max

D = 128
BANK = 512
BPB = BANK // D
MASK = 1.0e9
COS_EPS = 1e-7
LN_EPS = 1e-5
TINY = 1e-30
PRODUCT_SAFE = 0.7
LOWEST = -3.4028234e38

EARLY = {"f1": None, "f2": None, "W1": D, "W2": D, "ident": D, "bm": 1, "bih": 3, "bhh": 3, "beta": 1}
LATE = {"WmT": D, "WihT": 3 * D, "WhhT": 3 * D, "Ws": D, "Wn": D}


def columns_of(names, NB):
    at, where = 0, {}
    for name, width in names.items():
        where[name] = (at, NB if width is None else width)
        at += where[name][1]
    return where, at


def build(nc, x_rows, adjT, adj, early, late, out):
    N = adj.shape[0]
    NB = N // D
    BK = N // BANK
    HALF = N // 2
    HBK = BK // 2
    SPAN = NB // 2
    KEPT_AT = (0, SPAN // 2)
    NKEPT = 4
    RING = 4
    TILES = 2 * NB
    CH = 1024
    NCH = N // CH
    NSB = NB // 2
    NBATCH = NB // 2
    LEAD = 4
    HIGH_BY_DVE = (1, 7, 11, 15)

    early_at, early_width = columns_of(EARLY, NB)
    late_at, late_width = columns_of(LATE, NB)

    with ExitStack() as ctx:
        def sb(name, shape, dt=F32):
            return ctx.enter_context(nc.sbuf_tensor(name, shape, dt))

        def sb_over(name, shape, dt, base):
            return nc.alloc_sbuf_tensor_at(name, shape, dt, offset=base)

        def next_base():
            return -(-nc.sbuf_base // 32) * 32

        def sem(name):
            return ctx.enter_context(nc.semaphore(name))

        par = sb("par", [D, early_width])
        xrow = sb("xrow", [D, N])
        yH = sb("yH", [D, N], F32R)
        yL = sb("yL", [D, N], F32R)
        xT = sb("xT", [D, max(N, 5 * BANK)])
        raw = sb("raw", [D, RING, HALF])
        split_base = next_base()
        aH = sb("aH", [D, 2, HALF], F32R)
        aL = sb("aL", [D, 2, HALF], F32R)
        kept = sb("kept", [D, NKEPT, N])
        wH = sb("wH", [D, 2, D], F32R)
        wL = sb("wL", [D, 2, D], F32R)
        pt_base = next_base()
        ptH = sb("ptH", [D, 2, BANK], F32R)
        ptL = sb("ptL", [D, 2, BANK], F32R)
        oT = sb("oT", [D, 2 * D])
        lpar = sb_over("lpar", [D, late_width], F32, pt_base)
        scratch = sb_over("scratch", [D, 5, BANK], F32, split_base)
        s1 = sb("s1", [D, NB])
        s2 = sb("s2", [D, NB])
        s3 = sb("s3", [D, NB])
        mean = sb("mean", [D, NB])
        rstd = sb("rstd", [D, NB])
        unorm = sb("unorm", [D, NB])
        epsu = sb("epsu", [D, NB])
        degp = sb("degp", [D, NB, 2])
        rdeg = sb("rdeg", [D, NB])
        cmax = sb("cmax", [D, 2, NCH])
        nmax = sb("nmax", [D, NB])
        psums = sb("psums", [D, NB, NCH])
        rsum = sb("rsum", [D, 2])
        umax = sb("umax", [D, 2])
        flag = sb("flag", [D, 1], I32)
        bsum = sb("bsum", [D, 2])
        ps = ctx.enter_context(nc.psum_tensor("ps", [D, 8, BANK], F32))

        def p(name, a=0, b=None):
            t, (at, w) = (par, early_at[name]) if name in EARLY else (lpar, late_at[name])
            return t[:, at + a:at + (w if b is None else b)]

        ident = p("ident")
        rowbuf = raw[:, :, :].rearrange("p (s a) c -> p s (a c)", s=2)
        unitH = aH[:, :, :].rearrange("p a c -> p (a c)")
        unitL = aL[:, :, :].rearrange("p a c -> p (a c)")
        gT0, z0 = [xT[:, i * BANK:(i + 1) * BANK] for i in range(3)], [xT[:, i * BANK:(i + 1) * BANK] for i in (3, 4)]
        gT = [scratch[:, i, :] for i in range(3)]
        w12 = par[:, early_at["W1"][0]:early_at["W1"][0] + 2 * D]
        tmp = w12.rearrange("p (a d) -> p a d", d=D)
        stats = w12[:, 0:NB * 6].rearrange("p (b s) -> p b s", s=6)
        ones = oT[:, 0:D]
        S_BANKS, PT_BANKS, O_BANK, OT_BANK = (0, 2), (4, 5), 6, 7
        S2 = [ps[:, s:s + 2, :].rearrange("p a c -> p (a c)") for s in S_BANKS]

        BY_ACT = [k for k in range(NBATCH) if k not in HIGH_BY_DVE]

        def chunk(t, c):
            return t[:, c * BANK:(c + 1) * BANK]

        in_landed = sem("in_landed")
        late_landed = sem("late_landed")
        tile_landed = [sem(f"tile_landed{s}") for s in range(RING)]
        kept_landed = [sem(f"kept_landed{k}") for k in range(NKEPT)]
        aH_ready = sem("aH_ready")
        aL_ready = sem("aL_ready")
        tile_used = sem("tile_used")
        aH_used = sem("aH_used")
        w_ready = sem("w_ready")
        bank_done = sem("bank_done")
        g_ready = sem("g_ready")
        proj_done = sem("proj_done")
        z_ready = sem("z_ready")
        yH_ready = sem("yH_ready")
        yL_ready = sem("yL_ready")
        t_ready = sem("t_ready")
        dve_step = sem("dve_step")
        var_ready = sem("var_ready")
        root_ready = sem("root_ready")
        x_ready = sem("x_ready")
        sq_ready = sem("sq_ready")
        unit_ready = sem("unit_ready")
        unitT_done = sem("unitT_done")
        unitH_ready = sem("unitH_ready")
        unitL_ready = sem("unitL_ready")
        diag_ready = sem("diag_ready")
        uspread_done = sem("uspread_done")
        urow_ready = sem("urow_ready")
        umax_ready = sem("umax_ready")
        umax_all = sem("umax_all")
        row_landed = [sem(f"row_landed{r}") for r in range(2)]
        deg_done = sem("deg_done")
        bias_ready = sem("bias_ready")
        bw_step = sem("bw_step")
        bw_ready = sem("bw_ready")
        s_ready = sem("s_ready")
        m_ready = sem("m_ready")
        max_ready = sem("max_ready")
        exp_done = sem("exp_done")
        pt_ready = sem("pt_ready")
        ptH_ready = sem("ptH_ready")
        ptH_own = sem("ptH_own")
        ptL_ready = sem("ptL_ready")
        pv_done = sem("pv_done")
        o_copied = sem("o_copied")
        o_turned = sem("o_turned")
        o_step = sem("o_step")
        o_done = sem("o_done")
        xT_done = sem("xT_done")
        xT_ready = sem("xT_ready")
        self_done = sem("self_done")
        msg_done = sem("msg_done")
        msg_ready = sem("msg_ready")
        gates_done = sem("gates_done")
        r_ready = sem("r_ready")
        zg_ready = sem("zg_ready")
        narg_ready = sem("narg_ready")
        n_ready = sem("n_ready")
        gru_step = sem("gru_step")
        gru_ready = sem("gru_ready")
        gruT_done = sem("gruT_done")
        ones_ready = sem("ones_ready")
        out_written = sem("out_written")
        waits_passed = sem("waits_passed")

        block = ctx.enter_context(nc.Block())

        def rounds(eng, n, peel):
            yield from range(peel)
            if n > peel:
                with eng.Fori(peel, n) as it:
                    yield it

        def wait_alone(eng, semaphore, value):
            eng.wait_ge(semaphore, value)
            if not isinstance(value, int):
                eng.sem_inc(waits_passed, 1)

        def wait_bank(eng, pass_index, b):
            h, j = divmod(b, HBK)
            if j == HBK - 1:
                eng.wait_ge(tile_used, (pass_index + 1) * TILES - 1 + h)
            else:
                eng.wait_ge(bank_done, pass_index * (BK - 2) + h * (HBK - 1) + j + 1)

        @block.sync
        def _(sp):
            sp.dma_start(xrow[:], x_rows).then_inc(in_landed, 16)
            sp.dma_start(par[:], early).then_inc(in_landed, 16)
            adjT_tiles = adjT.rearrange("(b q) (h c) -> b h q c", q=D, h=2)
            adjT_blocks = adjT.rearrange("(b q) c -> b q c", q=D)
            adj_rows = adj.rearrange("(b q) c -> b q c", q=D)
            streamed = [(k, h) for k in range(SPAN) if k not in KEPT_AT for h in range(2)]

            def load_kept():
                for n in range(NKEPT):
                    b = SPAN * (n // 2) + KEPT_AT[n % 2]
                    sp.dma_start(kept[:, n, :], adjT_blocks[b]).then_inc(kept_landed[n], 16)

            def stream(ps_index):
                base = ps_index * TILES
                for it in rounds(sp, 2, 2 if ps_index == 0 else 0):
                    for s, (k, h) in enumerate(streamed):
                        before = s - RING
                        k0, h0 = streamed[before]
                        count = 2 * k0 + h0 + 1 - (2 * SPAN if before < 0 else 0)
                        if not (ps_index == 0 and isinstance(it, int) and it == 0 and before < 0):
                            sp.wait_ge(aL_ready, it * (2 * SPAN) + (base + count))
                        sp.dma_start(raw[:, s % RING, :], adjT_tiles[it * SPAN + k, h]).then_inc(tile_landed[s % RING], 16)

            load_kept()
            for q in range(4):
                stream(q)
            sp.wait_ge(aL_ready, 4 * TILES)
            for r in range(2):
                sp.dma_start(rowbuf[:, r, :], adj_rows[r]).then_inc(row_landed[r], 16)
            with sp.Fori(1, NSB) as sbi:
                for r in range(2):
                    sp.wait_ge(m_ready, sbi * (2 * NCH) + (r + 1 - 2) * NCH)
                    sp.dma_start(rowbuf[:, r, :], adj_rows[sbi * 2 + r]).then_inc(row_landed[r], 16)
            sp.wait_ge(m_ready, NB * NCH)
            sp.wait_ge(pv_done, NSB * NBATCH)
            sp.dma_start(lpar[:], late).then_inc(late_landed, 16)
            load_kept()
            stream(4)
            stream(5)
            out_blocks = out.rearrange("(b q) d -> q b d", q=D)
            for c in range(BK):
                sp.wait_ge(x_ready, 3 * BK + c + 1)
                sp.dma_start(out_blocks[:, c * BPB:(c + 1) * BPB, :],
                             chunk(xrow, c).rearrange("p (b d) -> p b d", d=D)).then_inc(out_written, 16)
            sp.wait_ge(out_written, 16 * BK)

        @block.gpsimd
        def _(pool):
            def stage(pass_index, split):
                pool.wait_ge(yL_ready, (split + 1) * BK)
                for it in rounds(pool, NB // 2, 1 if pass_index == 0 else 0):
                    for r in range(2):
                        b = it * 2 + r
                        first = pass_index == 0 and isinstance(it, int) and it == 0
                        if not first:
                            pool.wait_ge(tile_used, it * 4 + (pass_index * TILES + 2 * r - 2))
                        pool.tensor_copy(wH[:, r, :], yH[:, bass.ts(b, D)].bitcast(F32))
                        pool.tensor_copy(wL[:, r, :], yL[:, bass.ts(b, D)].bitcast(F32)).then_inc(w_ready, 1)

            nc.gpsimd.memset(ones, 1.0).then_inc(ones_ready, 1)
            for q in range(4):
                stage(q, q)

            pool.wait_ge(umax_ready, 1)
            pool.partition_all_reduce(umax[:, 1:2], umax[:, 0:1], D, RMAX).then_inc(umax_all, 1)
            pool.wait_ge(unitL_ready, BK)
            pool.wait_ge(tile_used, 4 * TILES)

            def stage_unit(rb, r, nth):
                if nth is not None:
                    pool.wait_ge(s_ready, nth)
                c = bass.ts(rb, D)
                pool.tensor_tensor(tmp[:, 0, :], unitH[:, c].bitcast(F32), unitL[:, c].bitcast(F32), ALU.add).then_inc(bw_step, 1)
                wait_alone(pool, bw_step, rb * 3 + 1)
                if not (isinstance(rb, int) and rb == 0):
                    wait_alone(pool, bw_ready, rb)
                pool.tensor_scalar(tmp[:, 1, :], tmp[:, 0, :], p("beta"), 0.0, ALU.mult, ALU.add).then_inc(bw_step, 1)
                wait_alone(pool, bw_step, rb * 3 + 2)
                pool.tensor_copy(wH[:, r, :], tmp[:, 1, :]).then_inc(bw_step, 1)
                wait_alone(pool, bw_step, rb * 3 + 3)
                pool.tensor_tensor(wL[:, r, :], tmp[:, 1, :], wH[:, r, :].bitcast(F32), ALU.subtract).then_inc(bw_ready, 1)

            def mask_bias(rb, r):
                for h in range(2):
                    wait_alone(pool, deg_done, rb * 2 + h + 1)
                    t = rowbuf[:, r, h * HALF:(h + 1) * HALF]
                    pool.tensor_scalar(t, t, -1.0, MASK, ALU.add, ALU.mult).then_inc(bias_ready, 1)

            for r in range(2):
                stage_unit(r, r, None)
                mask_bias(r, r)
            with pool.Fori(1, NSB) as sbi:
                for r in range(2):
                    stage_unit(sbi * 2 + r, r, sbi * (2 * NCH) + (r + 1 - 2) * NCH)
                    mask_bias(sbi * 2 + r, r)
            stage(4, 5)
            stage(5, 6)

        @block.scalar
        def _(act):
            def split_high(pass_index):
                base = pass_index * TILES
                phase = pass_index if pass_index < 4 else pass_index - 4
                for it in rounds(act, 2, 2):
                    s = 0
                    for k in range(SPAN):
                        for h in range(2):
                            tile = 2 * SPAN * it + 2 * k + h
                            if k in KEPT_AT:
                                n = 2 * it + KEPT_AT.index(k)
                                src = kept[:, n, h * HALF:(h + 1) * HALF]
                                if phase == 0 and h == 0:
                                    act.wait_ge(kept_landed[n], 16 * (1 if pass_index < 4 else 2))
                            else:
                                src = raw[:, s % RING, :]
                                uses = 2 * len(range(s % RING, 2 * (SPAN - 2), RING))
                                nth = pass_index * uses + it * (uses // 2) + s // RING + 1
                                act.wait_ge(tile_landed[s % RING], 16 * nth)
                                s += 1
                            if base + tile >= 2:
                                act.wait_ge(aH_used, base + tile - 1)
                                act.wait_ge(aL_ready, base + tile - 1)
                            nc.scalar.activation(aH[:, h, :], src, ACT.Copy).then_inc(aH_ready, 1)

            def high(c, src, split):
                nc.scalar.activation(chunk(yH, c), src, ACT.Copy).then_inc(yH_ready, 1)

            def project(tq, pass_index, func):
                for step in range(BK + 2):
                    b = step
                    if b < BK:
                        wait_bank(act, pass_index, b)
                        if tq * BK + b >= 3:
                            act.wait_ge(proj_done, tq * BK + b - 2)
                        nc.scalar.activation(gT0[b % 3], ps[:, b, :], func).then_inc(g_ready, 1)
                    c = step - 2
                    if c >= 0 and tq < 3:
                        if tq == 1:
                            act.wait_ge(proj_done, tq * BK + c + 1)
                            high(c, ps[:, c, :], tq + 1)
                        else:
                            zn = (tq // 2) * BK + c
                            act.wait_ge(z_ready, zn + 1)
                            high(c, z0[c % 2], tq + 1)

            def root(n):
                act.wait_ge(var_ready, n + 1)
                nc.scalar.activation(s2[:], s1[:], ACT.Sqrt).then_inc(root_ready, 1)

            act.wait_ge(in_landed, 32)
            for c in range(BK):
                high(c, chunk(xrow, c), 0)
            for q in range(3):
                split_high(q)
                project(q, q, ACT.Relu if q == 1 else ACT.Copy)
            split_high(3)
            project(3, 3, ACT.Copy)
            root(0)

            for c in range(BK):
                act.wait_ge(x_ready, c + 1)
                high(c, chunk(xrow, c), 4)
                nc.scalar.activation(chunk(kept[:, 2, :], c), chunk(xrow, c), ACT.Square).then_inc(sq_ready, 1)
            root(1)
            for c in range(BK):
                act.wait_ge(unitT_done, c + 1)
                nc.scalar.activation(chunk(unitH, c), ps[:, c, :], ACT.Copy).then_inc(unitH_ready, 1)
            for c in range(BK):
                act.wait_ge(uspread_done, c + 1)
                nc.scalar.activation(chunk(xT, c), ps[:, c, :], ACT.Copy).then_inc(urow_ready, 1)

            def degrees(rb, r, h, sbi):
                if h == 0:
                    act.wait_ge(row_landed[r], sbi * 16 + 16)
                t = rowbuf[:, r, h * HALF:(h + 1) * HALF]
                nc.scalar.activation(t, t, ACT.Copy, accum_out=degp[:, bass.ds(rb, 1), h]).then_inc(deg_done, 1)

            def exponent(rb, slot, c):
                if c == 0:
                    act.wait_ge(max_ready, rb + 1)
                t = kept[:, slot, c * CH:(c + 1) * CH]
                nc.scalar.activation(t, t, ACT.Exp, bias=nmax[:, bass.ds(rb, 1)],
                                     accum_out=psums[:, bass.ds(rb, 1), c]).then_inc(exp_done, 1)

            def turned_high(sbi, k):
                n = sbi * NBATCH + k
                act.wait_ge(pt_ready, n + 1)
                if not (isinstance(sbi, int) and sbi == 0 and k < 2):
                    act.wait_ge(pv_done, n - 1)
                nc.scalar.activation(ptH[:, k % 2, :], ps[:, PT_BANKS[k % 2], :], ACT.Copy).then_inc(ptH_ready, 1)

            def o_copy(sbi):
                act.wait_ge(pv_done, sbi * NBATCH + NBATCH)
                nc.scalar.activation(oT[:], ps[:, O_BANK, 0:2 * D], ACT.Copy).then_inc(o_copied, 1)

            def super_block(sbi, parity, more, before):
                nxt = sbi + 1
                first_r0, first_r1 = 2 * NCH + 1 - LEAD, 4 * NCH + 1 - LEAD
                for k in range(NBATCH):
                    if k == 0 and before:
                        o_copy(sbi - 1)
                    if k not in HIGH_BY_DVE:
                        turned_high(sbi, k)
                    if k + NBATCH - first_r1 < NCH and before:
                        exponent(sbi * 2 + 1, 2 * parity + 1, k + NBATCH - first_r1)
                    if first_r0 <= k < first_r0 + NCH and more >= 1:
                        exponent(nxt * 2, 2 * (1 - parity), k - first_r0)
                    if k >= first_r1 and more >= 1:
                        exponent(nxt * 2 + 1, 2 * (1 - parity) + 1, k - first_r1)
                    if k in (1, 3) and more >= 1:
                        degrees(nxt * 2 + 1, 1, k // 2, nxt)
                    if k in (9, 11) and more == 2:
                        degrees((nxt + 1) * 2, 0, (k - 9) // 2, nxt + 1)

            for r in range(2):
                for h in range(2):
                    degrees(r, r, h, 0)
            for r in range(2):
                for c in range(NCH):
                    exponent(r, r, c)
            for h in range(2):
                degrees(2, 0, h, 1)
            super_block(0, 0, 2, False)
            with act.Fori(0, (NSB - 4) // 2) as it:
                super_block(it * 2 + 1, 1, 2, True)
                super_block(it * 2 + 2, 0, 2, True)
            super_block(NSB - 3, 1, 2, True)
            super_block(NSB - 2, 0, 1, True)
            super_block(NSB - 1, 1, 0, True)
            o_copy(NSB - 1)
            root(2)

            for c in range(BK):
                act.wait_ge(x_ready, BK + c + 1)
                high(c, chunk(xrow, c), 5)
            for c in range(BK):
                act.wait_ge(xT_done, c + 1)
                nc.scalar.activation(chunk(xT, c), ps[:, c, :], ACT.Copy).then_inc(xT_ready, 1)
            split_high(4)
            for c in range(BK):
                wait_bank(act, 4, c)
                nc.scalar.activation(chunk(xrow, c), ps[:, c, :], ACT.Copy).then_inc(g_ready, 1)
            for c in range(BK):
                act.wait_ge(msg_done, c + 1)
                nc.scalar.activation(scratch[:, 3, :], ps[:, 0, :], ACT.Relu, bias=p("bm")).then_inc(msg_ready, 1)
                act.wait_ge(gates_done, c + 1)
                nc.scalar.activation(scratch[:, 4, :], ps[:, 1, :], ACT.Sigmoid, bias=bsum[:, 0:1]).then_inc(r_ready, 1)
                nc.scalar.activation(gT[1], ps[:, 2, :], ACT.Sigmoid, bias=bsum[:, 1:2]).then_inc(zg_ready, 1)
                act.wait_ge(narg_ready, c + 1)
                nc.scalar.activation(gT[2], chunk(xrow, c), ACT.Tanh, bias=p("bih", 2, 3)).then_inc(n_ready, 1)
            root(3)

            for c in range(BK):
                act.wait_ge(x_ready, 2 * BK + c + 1)
                high(c, chunk(xrow, c), 6)
            for c in range(BK):
                act.wait_ge(xT_done, BK + c + 1)
                if c >= 3:
                    act.wait_ge(self_done, c - 2)
                nc.scalar.activation(gT[c % 3], ps[:, c, :], ACT.Copy).then_inc(xT_ready, 1)
            act.wait_ge(self_done, BK)
            split_high(5)
            act.wait_ge(tile_used, 6 * TILES - 1)
            for b in range(BK):
                wait_bank(act, 5, b)
                if b >= 3:
                    act.wait_ge(proj_done, 4 * BK + b - 2)
                nc.scalar.activation(gT[b % 3], ps[:, b, :], ACT.Copy).then_inc(g_ready, 1)
            root(4)

        @block.vector
        def _(dve):
            chain = [0]

            def link(ins):
                chain[0] += 1
                ins.then_inc(dve_step, 1)
                dve.wait_ge(dve_step, chain[0])

            def split_low(pass_index):
                base = pass_index * TILES
                for it in rounds(dve, 2, 2):
                    s = 0
                    for k in range(SPAN):
                        for h in range(2):
                            if k in KEPT_AT:
                                src = kept[:, 2 * it + KEPT_AT.index(k), h * HALF:(h + 1) * HALF]
                            else:
                                src = raw[:, s % RING, :]
                                s += 1
                            tile = 2 * SPAN * it + 2 * k + h
                            if base + tile >= 2:
                                dve.wait_ge(tile_used, base + tile - 1)
                            dve.wait_ge(aH_ready, base + tile + 1)
                            dve.tensor_tensor(aL[:, h, :], src, aH[:, h, :].bitcast(F32), ALU.subtract).then_inc(aL_ready, 1)

            def low(c, src, split):
                dve.wait_ge(yH_ready, split * BK + c + 1)
                dve.tensor_tensor(chunk(yL, c), src, chunk(yH, c).bitcast(F32), ALU.subtract).then_inc(yL_ready, 1)

            def project(tq):
                for step in range(BK + 1):
                    c = step
                    if c < BK and tq != 1:
                        zn = (tq // 2) * BK + c
                        dve.wait_ge(proj_done, tq * BK + c + 1)
                        if zn >= 2:
                            dve.wait_ge(yL_ready, (tq + 1) * BK + c - 1 if c >= 2 else tq * BK + BK)
                        filt = p("f1" if tq == 0 else "f2", c * BPB, (c + 1) * BPB)
                        dve.tensor_tensor(z0[c % 2].rearrange("p (b d) -> p b d", d=D),
                                          ps[:, c, :].rearrange("p (b d) -> p b d", d=D),
                                          filt.unsqueeze(2).to_broadcast([D, BPB, D]), ALU.mult).then_inc(z_ready, 1)
                    c = step - 1
                    if c >= 0:
                        if tq == 1:
                            low(c, ps[:, c, :], tq + 1)
                        else:
                            dve.wait_ge(z_ready, (tq // 2) * BK + c + 1)
                            low(c, z0[c % 2], tq + 1)

            def newton_root(n):
                dve.wait_ge(root_ready, n + 1)
                link(dve.reciprocal(s3[:], s2[:]))
                link(dve.tensor_tensor(s3[:], s3[:], s1[:], ALU.mult))
                link(dve.tensor_tensor(s3[:], s3[:], s2[:], ALU.add))
                link(dve.tensor_scalar(s2[:], s3[:], 0.5, None, ALU.mult))

            def layernorm(ready, value, nroot):
                dve.wait_ge(ready, value)
                with dve.Fori(0, NB) as b:
                    dve.bn_stats(stats[:, bass.ds(b, 1), :], xrow[:, bass.ts(b, D)]).then_inc(dve_step, 1)
                chain[0] += NB
                dve.wait_ge(dve_step, chain[0])
                mean_e, mean_o = stats[:, :, 1], stats[:, :, 4]
                m2_e, m2_o = stats[:, :, 2], stats[:, :, 5]
                link(dve.tensor_tensor(s1[:], m2_e, m2_o, ALU.add))
                link(dve.tensor_tensor(s2[:], mean_e, mean_o, ALU.subtract))
                link(dve.tensor_tensor(s3[:], mean_e, mean_o, ALU.add))
                link(dve.tensor_scalar(mean[:], s3[:], 0.5, None, ALU.mult))
                link(dve.scalar_tensor_tensor(out=s2[:], in0=s2[:], scalar=0.25, in1=s2[:], op0=ALU.mult, op1=ALU.mult))
                link(dve.scalar_tensor_tensor(out=s1[:], in0=s1[:], scalar=1.0 / D, in1=s2[:], op0=ALU.mult, op1=ALU.add))
                dve.tensor_scalar(s1[:], s1[:], LN_EPS, None, ALU.add).then_inc(var_ready, 1)
                newton_root(nroot)
                link(dve.reciprocal(rstd[:], s2[:]))
                with dve.Fori(0, BK) as c:
                    for i in range(BPB):
                        t = xrow[:, bass.ds(c * BANK + i * D, D)]
                        b = c * BPB + i
                        ins = dve.tensor_scalar(t, t, mean[:, bass.ds(b, 1)], rstd[:, bass.ds(b, 1)], ALU.subtract, ALU.mult)
                    ins.then_inc(x_ready, 1)

            dve.wait_ge(in_landed, 32)
            dve.tensor_tensor(bsum[:], p("bih", 0, 2), p("bhh", 0, 2), ALU.add).then_inc(gru_step, 1)
            for c in range(BK):
                low(c, chunk(xrow, c), 0)
            for q in range(3):
                split_low(q)
                project(q)
            split_low(3)
            for c in range(BK):
                dve.wait_ge(proj_done, 3 * BK + c + 1)
                dve.tensor_tensor(chunk(xrow, c), ps[:, c, :], chunk(xrow, c), ALU.add).then_inc(t_ready, 1)
            layernorm(t_ready, BK, 0)

            for c in range(BK):
                dve.wait_ge(x_ready, c + 1)
                low(c, chunk(xrow, c), 4)
            for c in range(BK):
                dve.wait_ge(sq_ready, c + 1)
                link(dve.tensor_reduce(s1[:, c * BPB:(c + 1) * BPB],
                                       chunk(kept[:, 2, :], c).rearrange("p (b d) -> p b d", d=D), AX.X, ALU.add))
            dve.tensor_scalar(s1[:], s1[:], TINY, None, ALU.max).then_inc(var_ready, 1)
            newton_root(1)
            link(dve.reciprocal(unorm[:], s2[:]))
            dve.tensor_reduce(umax[:, 0:1], unorm[:], AX.X, ALU.max).then_inc(umax_ready, 1)
            link(dve.tensor_scalar(epsu[:], unorm[:], COS_EPS, None, ALU.mult))
            for c in range(BK):
                ub = unorm[:, c * BPB:(c + 1) * BPB].unsqueeze(2).to_broadcast([D, BPB, D])
                dve.tensor_tensor(chunk(kept[:, 3, :], c).rearrange("p (b d) -> p b d", d=D),
                                  chunk(xrow, c).rearrange("p (b d) -> p b d", d=D), ub, ALU.mult).then_inc(unit_ready, 1)
                dve.tensor_tensor(chunk(kept[:, 2, :], c).rearrange("p (b d) -> p b d", d=D),
                                  ident.unsqueeze(1).to_broadcast([D, BPB, D]), ub, ALU.mult).then_inc(diag_ready, 1)
            for c in range(BK):
                dve.wait_ge(unitH_ready, c + 1)
                dve.tensor_tensor(chunk(unitL, c), ps[:, c, :], chunk(unitH, c).bitcast(F32), ALU.subtract).then_inc(unitL_ready, 1)
            dve.wait_ge(umax_all, 1)
            link(dve.tensor_scalar(flag[:], umax[:, 1:2], PRODUCT_SAFE, None, ALU.is_gt))
            small_norms = dve.value_load(flag[0:1, 0:1], min_val=0, max_val=1)
            dve.wait_ge(urow_ready, BK)

            def mask(rb, r, slot, c):
                n = rb * NCH + c
                with dve.If(small_norms > 0):
                    dve.wait_ge(s_ready, n + 1)
                    corr = kept[:, slot, c * CH:(c + 1) * CH]
                    dve.tensor_scalar(corr, xT[:, c * CH:(c + 1) * CH], epsu[:, bass.ds(rb, 1)], 1.0, ALU.mult, ALU.add)
                    dve.drain()
                    dve.reciprocal(corr, corr)
                    dve.drain()
                    dve.tensor_tensor(S2[c % 2], S2[c % 2], corr, ALU.mult)
                    dve.drain()
                wait_alone(dve, s_ready, n + 1)
                if c in (0, NCH // 2):
                    wait_alone(dve, bias_ready, rb * 2 + c // (NCH // 2) + 1)
                dve.tensor_tensor_reduce(kept[:, slot, c * CH:(c + 1) * CH], S2[c % 2], rowbuf[:, r, c * CH:(c + 1) * CH],
                                         1.0, LOWEST, ALU.add, ALU.max, cmax[:, r, c:c + 1]).then_inc(m_ready, 1)
                if c == NCH - 1:
                    dve.wait_ge(m_ready, n + 1)
                    dve.tensor_reduce(nmax[:, bass.ds(rb, 1)], cmax[:, r, :], AX.X, ALU.max,
                                      negate=True).then_inc(max_ready, 1)

            def turned_low(sbi, k):
                if k in HIGH_BY_DVE:
                    own = HIGH_BY_DVE.index(k)
                    dve.wait_ge(pt_ready, sbi * NBATCH + k + 1)
                    if not (isinstance(sbi, int) and sbi == 0 and k < 2):
                        dve.wait_ge(pv_done, sbi * NBATCH + (k - 1))
                    dve.tensor_copy(ptH[:, k % 2, :], ps[:, PT_BANKS[k % 2], :]).then_inc(ptH_own, 1)
                    dve.wait_ge(ptH_own, sbi * len(HIGH_BY_DVE) + (own + 1))
                else:
                    dve.wait_ge(ptH_ready, sbi * len(BY_ACT) + (BY_ACT.index(k) + 1))
                dve.tensor_tensor(ptL[:, k % 2, :], ps[:, PT_BANKS[k % 2], :], ptH[:, k % 2, :].bitcast(F32),
                                  ALU.subtract).then_inc(ptL_ready, 1)

            def o_rows(sbi):
                rows = bass.ds(sbi * 2, 2)
                dve.wait_ge(o_turned, sbi + 1)
                dve.tensor_reduce(rsum[:], psums[:, rows, :], AX.X, ALU.add).then_inc(o_step, 1)
                dve.wait_ge(o_step, sbi * 2 + 1)
                dve.reciprocal(rsum[:], rsum[:]).then_inc(o_step, 1)
                dve.wait_ge(o_step, sbi * 2 + 2)
                for r in range(2):
                    b = sbi * 2 + r
                    t = xrow[:, bass.ts(b, D)]
                    ins = dve.scalar_tensor_tensor(out=t, in0=ps[:, OT_BANK, r * D:(r + 1) * D], scalar=rsum[:, r:r + 1],
                                                   in1=t, op0=ALU.mult, op1=ALU.add)
                ins.then_inc(o_done, 1)

            def mask_chunk(sbi, parity, m):
                r, c = divmod(m, NCH)
                mask(sbi * 2 + r, r, 2 * parity + r, c)

            def super_block(sbi, parity, more, before):
                for k in range(NBATCH):
                    m = (k + LEAD - 2) // 2
                    if k % 2 == 0 and m < 2 * NCH and more >= 1:
                        mask_chunk(sbi + 1, 1 - parity, m)
                    if k % 2 == 0 and m >= 2 * NCH and more == 2:
                        mask_chunk(sbi + 2, parity, m - 2 * NCH)
                    turned_low(sbi, k)
                    if k == 3 and before:
                        o_rows(sbi - 1)

            for m in range(2 * NCH):
                mask_chunk(0, 0, m)
            mask_chunk(1, 1, 0)
            super_block(0, 0, 2, False)
            with dve.Fori(0, (NSB - 4) // 2) as it:
                super_block(it * 2 + 1, 1, 2, True)
                super_block(it * 2 + 2, 0, 2, True)
            super_block(NSB - 3, 1, 2, True)
            super_block(NSB - 2, 0, 1, True)
            super_block(NSB - 1, 1, 0, True)
            o_rows(NSB - 1)
            link(dve.tensor_reduce(rdeg[:], degp[:], AX.X, ALU.add))
            link(dve.tensor_scalar(rdeg[:], rdeg[:], 1.0, None, ALU.max))
            link(dve.reciprocal(rdeg[:], rdeg[:]))
            layernorm(o_done, NSB, 2)

            for c in range(BK):
                dve.wait_ge(x_ready, BK + c + 1)
                low(c, chunk(xrow, c), 5)
            split_low(4)
            dve.wait_ge(gru_step, 1)
            for c in range(BK):
                h = chunk(xT, c)
                rg, zg, ng, t = scratch[:, 4, :], gT[1], gT[2], gT[0]
                narg = chunk(xrow, c)
                g = 1 + 5 * c
                dve.wait_ge(r_ready, c + 1)
                dve.scalar_tensor_tensor(out=narg, in0=ps[:, 4, :], scalar=p("bhh", 2, 3), in1=rg,
                                         op0=ALU.add, op1=ALU.mult).then_inc(gru_step, 1)
                dve.wait_ge(gru_step, g + 1)
                dve.tensor_tensor(narg, narg, ps[:, 3, :], ALU.add).then_inc(narg_ready, 1)
                dve.wait_ge(n_ready, c + 1)
                dve.tensor_tensor(t, h, ng, ALU.subtract).then_inc(gru_step, 1)
                dve.wait_ge(gru_step, g + 2)
                dve.wait_ge(zg_ready, c + 1)
                dve.tensor_tensor(t, t, zg, ALU.mult).then_inc(gru_step, 1)
                dve.wait_ge(gru_step, g + 3)
                dve.tensor_tensor(t, t, ng, ALU.add).then_inc(gru_step, 1)
                dve.wait_ge(gru_step, g + 4)
                dve.tensor_tensor(t, t, h, ALU.add).then_inc(gru_step, 1)
                dve.wait_ge(gruT_done, c + 1)
                dve.tensor_copy(chunk(xrow, c), ps[:, 5, :]).then_inc(t_ready, 1)
            layernorm(t_ready, 2 * BK, 3)

            for c in range(BK):
                dve.wait_ge(x_ready, 2 * BK + c + 1)
                low(c, chunk(xrow, c), 6)
            for c in range(BK):
                dve.wait_ge(self_done, c + 1)
                dve.tensor_tensor(chunk(xrow, c), ps[:, c, :], chunk(xrow, c), ALU.add).then_inc(gru_ready, 1)
            split_low(5)
            dve.wait_ge(gru_ready, BK)
            for c in range(BK):
                dve.wait_ge(proj_done, 4 * BK + c + 1)
                for i in range(BPB):
                    b = c * BPB + i
                    t = xrow[:, b * D:(b + 1) * D]
                    ins = dve.scalar_tensor_tensor(out=t, in0=ps[:, c, i * D:(i + 1) * D], scalar=rdeg[:, b:b + 1],
                                                   in1=t, op0=ALU.mult, op1=ALU.add)
                ins.then_inc(t_ready, 1)
            layernorm(t_ready, 3 * BK, 4)

        @block.tensor
        def _(pe):
            def multiply(pass_index):
                def tiles(it, first, last):
                    for r in range(2):
                        for h in range(2):
                            tile = 4 * it + (pass_index * TILES + 2 * r + h)
                            banks = [ps[:, h * HBK + j, :] for j in range(HBK)]
                            cols = [slice(j * BANK, (j + 1) * BANK) for j in range(HBK)]
                            if h == 0:
                                pe.wait_ge(w_ready, 2 * it + (pass_index * NB + r + 1))
                            pe.wait_ge(aH_ready, tile + 1)
                            for b, c in zip(banks, cols):
                                pe.matmul(b, wH[:, r, :], aH[:, h, c], start=first and r == 0, stop=False)
                            for b, c in zip(banks, cols):
                                ins = pe.matmul(b, wL[:, r, :], aH[:, h, c], start=False, stop=False)
                            ins.then_inc(aH_used, 1)
                            pe.wait_ge(aL_ready, tile + 1)
                            done = last and r == 1
                            for b, c in zip(banks, cols):
                                ins = pe.matmul(b, wH[:, r, :], aL[:, h, c], start=False, stop=done)
                                if done and c.stop < HALF:
                                    ins.then_inc(bank_done, 1)
                            ins.then_inc(tile_used, 1)
                tiles(0, True, False)
                with pe.Fori(1, NB // 2 - 1) as it:
                    tiles(it, False, False)
                tiles(NB // 2 - 1, False, True)

            def project(tq, weights, turned):
                for b in range(BK):
                    pe.wait_ge(g_ready, (tq if tq < 4 else 5) * BK + b + 1)
                    for i in range(BPB):
                        o, t = ps[:, b, i * D:(i + 1) * D], turned[b % 3][:, i * D:(i + 1) * D]
                        if weights is None:
                            ins = pe.transpose(o, t, ident)
                        else:
                            ins = pe.matmul(o, t, weights, start=True, stop=True)
                    ins.then_inc(proj_done, 1)

            def turn(src, ready, base, done):
                for c in range(BK):
                    pe.wait_ge(ready, base + c + 1)
                    for i in range(BPB):
                        ins = pe.transpose(ps[:, c, i * D:(i + 1) * D], src[:, c * BANK + i * D:c * BANK + (i + 1) * D], ident)
                    ins.then_inc(done, 1)

            pe.wait_ge(in_landed, 32)
            for q in range(4):
                multiply(q)
                project(q, [p("W1"), p("W2"), None, None][q], gT0)

            pe.wait_ge(t_ready, BK)
            turn(kept[:, 3, :], unit_ready, 0, unitT_done)
            pe.wait_ge(ones_ready, 1)
            for c in range(BK):
                pe.wait_ge(unitL_ready, c + 1)
                pe.wait_ge(diag_ready, c + 1)
                pe.matmul(ps[:, c, :], ones, chunk(kept[:, 2, :], c), start=True, stop=True).then_inc(uspread_done, 1)
            pe.wait_ge(urow_ready, BK)

            def scores(sbi, q):
                m, j = divmod(q, CH // BANK)
                r, c = divmod(m, NCH)
                if j == 0:
                    if c == 0:
                        pe.wait_ge(bw_ready, sbi * 2 + (r + 1))
                    if not (isinstance(sbi, int) and sbi == 0 and m < 2):
                        pe.wait_ge(m_ready, sbi * (2 * NCH) + (m - 1))
                o = ps[:, S_BANKS[c % 2] + j, :]
                col = slice(c * CH + j * BANK, c * CH + (j + 1) * BANK)
                pe.matmul(o, wH[:, r, :], unitH[:, col], start=True, stop=False)
                pe.matmul(o, wH[:, r, :], unitL[:, col], start=False, stop=False)
                ins = pe.matmul(o, wL[:, r, :], unitH[:, col], start=False, stop=True)
                if j == CH // BANK - 1:
                    ins.then_inc(s_ready, 1)

            def turn_batch(sbi, parity, k, first):
                n = sbi * NBATCH + k
                if k % (NBATCH // NCH) == 0:
                    pe.wait_ge(exp_done, sbi * (2 * NCH) + (NCH + k // (NBATCH // NCH) + 1))
                if not first:
                    pe.wait_ge(ptL_ready, n - 1)
                for a in range(2):
                    for r in range(2):
                        j = 2 * k + a
                        ins = pe.transpose(ps[:, PT_BANKS[k % 2], (2 * a + r) * D:(2 * a + r + 1) * D],
                                           kept[:, 2 * parity + r, j * D:(j + 1) * D], ident)
                ins.then_inc(pt_ready, 1)

            def sum_batch(sbi, k, before):
                n = sbi * NBATCH + k
                if k == 0 and before:
                    pe.wait_ge(o_copied, sbi)
                pe.wait_ge(ptL_ready, n + 1)
                o = ps[:, O_BANK, 0:2 * D]
                for a in range(2):
                    j = 2 * k + a
                    jc, cols = slice(j * D, (j + 1) * D), slice(a * 2 * D, (a + 1) * 2 * D)
                    pe.matmul(o, yH[:, jc], ptH[:, k % 2, cols], start=(j == 0), stop=False)
                    pe.matmul(o, yH[:, jc], ptL[:, k % 2, cols], start=False, stop=False)
                    ins = pe.matmul(o, yL[:, jc], ptH[:, k % 2, cols], start=False, stop=(j == NB - 1))
                ins.then_inc(pv_done, 1)

            def turn_sums(sbi, first):
                pe.wait_ge(o_copied, sbi + 1)
                if not first:
                    pe.wait_ge(o_done, sbi)
                for r in range(2):
                    ins = pe.transpose(ps[:, OT_BANK, r * D:(r + 1) * D], oT[:, r * D:(r + 1) * D], ident)
                ins.then_inc(o_turned, 1)

            def super_block(sbi, parity, more, before, second=False):
                for k in range(NBATCH):
                    turn_batch(sbi, parity, k, not before and k < 2)
                    if k < NBATCH - LEAD and more >= 1:
                        scores(sbi + 1, k + LEAD)
                    if k >= NBATCH - LEAD and more == 2:
                        scores(sbi + 2, k - NBATCH + LEAD)
                    if k >= 1:
                        sum_batch(sbi, k - 1, before)
                    if k == 2 and before:
                        turn_sums(sbi - 1, second)
                sum_batch(sbi, NBATCH - 1, before)

            for q in range(NBATCH):
                scores(0, q)
            for q in range(LEAD):
                scores(1, q)
            super_block(0, 0, 2, False)
            super_block(1, 1, 2, True, True)
            super_block(2, 0, 2, True)
            with pe.Fori(1, (NSB - 4) // 2) as it:
                super_block(it * 2 + 1, 1, 2, True)
                super_block(it * 2 + 2, 0, 2, True)
            super_block(NSB - 3, 1, 2, True)
            super_block(NSB - 2, 0, 1, True)
            super_block(NSB - 1, 1, 0, True)
            turn_sums(NSB - 1, False)

            pe.wait_ge(o_done, NSB)
            turn(xrow, x_ready, BK, xT_done)
            pe.wait_ge(xT_ready, BK)
            multiply(4)
            pe.wait_ge(late_landed, 16)
            pe.wait_ge(g_ready, 5 * BK)
            for c in range(BK):
                h, msg = chunk(xT, c), scratch[:, 3, :]
                pe.matmul(ps[:, 0, :], p("WmT"), chunk(xrow, c), start=True, stop=True).then_inc(msg_done, 1)
                pe.wait_ge(msg_ready, c + 1)
                if c >= 1:
                    pe.wait_ge(narg_ready, c)
                    pe.wait_ge(zg_ready, c)
                for gate in range(2):
                    w = slice(gate * D, (gate + 1) * D)
                    pe.matmul(ps[:, 1 + gate, :], p("WihT")[:, w], msg, start=True, stop=False)
                    pe.matmul(ps[:, 1 + gate, :], p("WhhT")[:, w], h, start=False, stop=True)
                pe.matmul(ps[:, 3, :], p("WihT", 2 * D), msg, start=True, stop=True)
                pe.matmul(ps[:, 4, :], p("WhhT", 2 * D), h, start=True, stop=True).then_inc(gates_done, 1)
                pe.wait_ge(gru_step, 1 + 5 * c + 5)
                if c >= 1:
                    pe.wait_ge(t_ready, BK + c)
                for i in range(BPB):
                    ins = pe.transpose(ps[:, 5, i * D:(i + 1) * D], gT[0][:, i * D:(i + 1) * D], ident)
                ins.then_inc(gruT_done, 1)

            pe.wait_ge(t_ready, 2 * BK)
            turn(xrow, x_ready, 2 * BK, xT_done)
            for c in range(BK):
                pe.wait_ge(xT_ready, BK + c + 1)
                for i in range(BPB):
                    ins = pe.matmul(ps[:, c, i * D:(i + 1) * D], gT[c % 3][:, i * D:(i + 1) * D], p("Ws"), start=True, stop=True)
                ins.then_inc(self_done, 1)
            pe.wait_ge(gru_ready, BK)
            multiply(5)
            project(4, p("Wn"), gT)


NAMES = ("x_rows", "adjT", "adj", "early", "late")


def kernel(x, adj, L0_gnn_W1, L0_gnn_f1, L0_gnn_W2, L0_gnn_f2, L1_gnn_beta, L2_gnn_W_msg, L2_gnn_b_msg, L2_gnn_W_ih,
           L2_gnn_W_hh, L2_gnn_b_ih, L2_gnn_b_hh, L3_gnn_W_self, L3_gnn_W_neigh):
    import numpy as np
    import concourse.bacc as bacc
    from concourse.bass_utils import run_bass_kernel_spmd

    x, adj = np.asarray(x), np.asarray(adj)
    N = x.shape[0]
    NB = N // D

    def columns(v, n):
        return np.asarray(v).reshape(n, D).T

    packed = {
        "f1": columns(L0_gnn_f1, NB), "f2": columns(L0_gnn_f2, NB),
        "W1": np.asarray(L0_gnn_W1), "W2": np.asarray(L0_gnn_W2), "WmT": np.asarray(L2_gnn_W_msg).T,
        "WihT": np.asarray(L2_gnn_W_ih).T, "WhhT": np.asarray(L2_gnn_W_hh).T,
        "Ws": np.asarray(L3_gnn_W_self), "Wn": np.asarray(L3_gnn_W_neigh), "ident": np.eye(D, dtype=np.float32),
        "bm": columns(L2_gnn_b_msg, 1), "bih": columns(L2_gnn_b_ih, 3), "bhh": columns(L2_gnn_b_hh, 3),
        "beta": np.broadcast_to(np.asarray(L1_gnn_beta).reshape(1, 1), (D, 1)),
    }
    early, late = (np.ascontiguousarray(np.concatenate([packed[name] for name in names], axis=1)) for names in (EARLY, LATE))
    x_rows = np.ascontiguousarray(x.reshape(NB, D, D).transpose(1, 0, 2).reshape(D, N))
    arrays = {"x_rows": x_rows, "adjT": np.ascontiguousarray(adj.T), "adj": np.ascontiguousarray(adj), "early": early, "late": late}

    nc = bacc.Bacc("TRN2", target_bir_lowering=False, num_devices=1)
    args = [nc.dram_tensor(n, arrays[n].shape, F32, kind="ExternalInput").ap() for n in NAMES]
    out = nc.dram_tensor("out", (N, D), F32, kind="ExternalOutput").ap()
    build(nc, *args, out)
    r = run_bass_kernel_spmd(nc, [arrays], core_ids=[0])
    return r.results[0]["out"]
```

```python
from contextlib import ExitStack

import concourse.bass as bass
from concourse import mybir

ALU = mybir.AluOpType
ACT = mybir.ActivationFunctionType
AX = mybir.AxisListType
F32 = mybir.dt.float32
F32R = mybir.dt.float32r
I32 = mybir.dt.int32
RMAX = bass.bass_isa.ReduceOp.max

D = 128
BANK = 512
BPB = BANK // D
MASK = 1.0e9
COS_EPS = 1e-7
LN_EPS = 1e-5
TINY = 1e-30
PRODUCT_SAFE = 0.7
LOWEST = -3.4028234e38

EARLY = {"f1": None, "f2": None, "W1": D, "W2": D, "ident": D, "bm": 1, "bih": 3, "bhh": 3, "beta": 1}
LATE = {"WmT": D, "WihT": 3 * D, "WhhT": 3 * D, "Ws": D, "Wn": D}


def columns_of(names, NB):
    at, where = 0, {}
    for name, width in names.items():
        where[name] = (at, NB if width is None else width)
        at += where[name][1]
    return where, at


def build(nc, x_rows, adjT, adj, early, late, out):
    N = adj.shape[0]
    NB = N // D
    BK = N // BANK
    HALF = N // 2
    HBK = BK // 2
    SPAN = NB // 2
    KEPT_AT = (0, SPAN // 2)
    NKEPT = 4
    RING = 4
    TILES = 2 * NB
    CH = 1024
    NCH = N // CH
    NSB = NB // 2
    NBATCH = NB // 2
    LEAD = 4
    HIGH_BY_DVE = (1, 7, 11, 15)

    early_at, early_width = columns_of(EARLY, NB)
    late_at, late_width = columns_of(LATE, NB)

    with ExitStack() as ctx:
        def sb(name, shape, dt=F32):
            return ctx.enter_context(nc.sbuf_tensor(name, shape, dt))

        def sb_over(name, shape, dt, base):
            return nc.alloc_sbuf_tensor_at(name, shape, dt, offset=base)

        def next_base():
            return -(-nc.sbuf_base // 32) * 32

        def sem(name):
            return ctx.enter_context(nc.semaphore(name))

        par = sb("par", [D, early_width])
        xrow = sb("xrow", [D, N])
        yH = sb("yH", [D, N], F32R)
        yL = sb("yL", [D, N], F32R)
        xT = sb("xT", [D, max(N, 5 * BANK)])
        raw = sb("raw", [D, RING, HALF])
        split_base = next_base()
        aH = sb("aH", [D, 2, HALF], F32R)
        aL = sb("aL", [D, 2, HALF], F32R)
        kept = sb("kept", [D, NKEPT, N])
        wH = sb("wH", [D, 2, D], F32R)
        wL = sb("wL", [D, 2, D], F32R)
        pt_base = next_base()
        ptH = sb("ptH", [D, 2, BANK], F32R)
        ptL = sb("ptL", [D, 2, BANK], F32R)
        oT = sb("oT", [D, 2 * D])
        lpar = sb_over("lpar", [D, late_width], F32, pt_base)
        scratch = sb_over("scratch", [D, 10, BANK], F32, split_base)
        s1 = sb("s1", [D, 2 * NB])
        s2 = sb("s2", [D, 2 * NB])
        s3 = sb("s3", [D, 2 * NB])
        mean = sb("mean", [D, NB])
        rstd = sb("rstd", [D, NB])
        unorm = sb("unorm", [D, NB])
        epsu = sb("epsu", [D, NB])
        degp = sb("degp", [D, NB, 2])
        rdeg = sb("rdeg", [D, NB])
        cmax = sb("cmax", [D, 2, NCH])
        nmax = sb("nmax", [D, NB])
        psums = sb("psums", [D, NB, NCH])
        rsum = sb("rsum", [D, 2])
        umax = sb("umax", [D, 2])
        flag = sb("flag", [D, 1], I32)
        bsum = sb("bsum", [D, 2])
        ps = ctx.enter_context(nc.psum_tensor("ps", [D, 8, BANK], F32))

        def p(name, a=0, b=None):
            t, (at, w) = (par, early_at[name]) if name in EARLY else (lpar, late_at[name])
            return t[:, at + a:at + (w if b is None else b)]

        ident = p("ident")
        rowbuf = raw[:, :, :].rearrange("p (s a) c -> p s (a c)", s=2)
        unitH = aH[:, :, :].rearrange("p a c -> p (a c)")
        unitL = aL[:, :, :].rearrange("p a c -> p (a c)")
        gT0, z0 = [xT[:, i * BANK:(i + 1) * BANK] for i in range(3)], [xT[:, i * BANK:(i + 1) * BANK] for i in (3, 4)]
        msg_s, r_s, z_s, n_s, g_s = [[scratch[:, 2 * i + j, :] for j in range(2)] for i in range(5)]
        tmp = p("W2")
        stats = par[:, 0:NB * 6].rearrange("p (b s) -> p b s", s=6)
        assert NB * 6 <= early_at["W2"][0]
        uT = kept[0:NB, 2, 0:D]
        S_BANKS, PT_BANKS, O_BANK, OT_BANK = (0, 2), (4, 5), 6, 7
        S2 = [ps[:, s:s + 2, :].rearrange("p a c -> p (a c)") for s in S_BANKS]

        BY_ACT = [k for k in range(NBATCH) if k not in HIGH_BY_DVE]

        def chunk(t, c):
            return t[:, c * BANK:(c + 1) * BANK]

        par_landed = sem("par_landed")
        x_landed = [sem(f"x_landed{h}") for h in range(2)]
        late_landed = sem("late_landed")
        tile_landed = [sem(f"tile_landed{s}") for s in range(RING)]
        kept_landed = [sem(f"kept_landed{k}") for k in range(NKEPT)]
        aH_ready = sem("aH_ready")
        aL_ready = sem("aL_ready")
        tile_used = sem("tile_used")
        aH_used = sem("aH_used")
        w_ready = sem("w_ready")
        bank_done = sem("bank_done")
        g_ready = sem("g_ready")
        proj_done = sem("proj_done")
        z_ready = sem("z_ready")
        yH_ready = sem("yH_ready")
        yL_ready = sem("yL_ready")
        t_ready = sem("t_ready")
        dve_step = sem("dve_step")
        var_ready = sem("var_ready")
        root_ready = sem("root_ready")
        x_ready = sem("x_ready")
        stats_ready = sem("stats_ready")
        unit_ready = sem("unit_ready")
        unitT_done = sem("unitT_done")
        unitH_ready = sem("unitH_ready")
        unitL_ready = sem("unitL_ready")
        unorm_ready = sem("unorm_ready")
        unormT_done = sem("unormT_done")
        uT_ready = sem("uT_ready")
        uspread_done = sem("uspread_done")
        urow_ready = sem("urow_ready")
        umax_ready = sem("umax_ready")
        umax_all = sem("umax_all")
        row_landed = [sem(f"row_landed{r}") for r in range(2)]
        deg_done = sem("deg_done")
        bias_ready = sem("bias_ready")
        bw_step = sem("bw_step")
        bw_ready = sem("bw_ready")
        s_ready = sem("s_ready")
        m_ready = sem("m_ready")
        max_ready = sem("max_ready")
        exp_done = sem("exp_done")
        pt_ready = sem("pt_ready")
        ptH_ready = sem("ptH_ready")
        ptH_own = sem("ptH_own")
        ptL_ready = sem("ptL_ready")
        pv_done = sem("pv_done")
        o_copied = sem("o_copied")
        o_turned = sem("o_turned")
        o_step = sem("o_step")
        o_done = sem("o_done")
        xT_done = sem("xT_done")
        xT_ready = sem("xT_ready")
        self_done = sem("self_done")
        msg_done = sem("msg_done")
        msg_ready = sem("msg_ready")
        r_done = sem("r_done")
        zg_done = sem("zg_done")
        hn_done = sem("hn_done")
        in_done = sem("in_done")
        r_ready = sem("r_ready")
        zg_ready = sem("zg_ready")
        narg_ready = sem("narg_ready")
        n_ready = sem("n_ready")
        hn_used = sem("hn_used")
        gru_step = sem("gru_step")
        gru_ready = sem("gru_ready")
        self_ready = sem("self_ready")
        sum_ready = sem("sum_ready")
        gruT_done = sem("gruT_done")
        out_written = sem("out_written")
        waits_passed = sem("waits_passed")

        block = ctx.enter_context(nc.Block())

        def rounds(eng, n, peel):
            yield from range(peel)
            if n > peel:
                with eng.Fori(peel, n) as it:
                    yield it

        def wait_alone(eng, semaphore, value):
            eng.wait_ge(semaphore, value)
            if not isinstance(value, int):
                eng.sem_inc(waits_passed, 1)

        def wait_bank(eng, pass_index, b):
            h, j = divmod(b, HBK)
            if j == HBK - 1:
                eng.wait_ge(tile_used, (pass_index + 1) * TILES - 1 + h)
            else:
                eng.wait_ge(bank_done, pass_index * (BK - 2) + h * (HBK - 1) + j + 1)

        @block.sync
        def _(sp):
            for h in range(2):
                cols = slice(h * HALF, (h + 1) * HALF)
                sp.dma_start(xrow[:, cols], x_rows[:, cols]).then_inc(x_landed[h], 16)
            adjT_tiles = adjT.rearrange("(b q) (h c) -> b h q c", q=D, h=2)
            adjT_blocks = adjT.rearrange("(b q) c -> b q c", q=D)
            adj_rows = adj.rearrange("(b q) c -> b q c", q=D)
            streamed = [(k, h) for k in range(SPAN) if k not in KEPT_AT for h in range(2)]

            def load_kept(which):
                for n in which:
                    b = SPAN * (n // 2) + KEPT_AT[n % 2]
                    sp.dma_start(kept[:, n, :], adjT_blocks[b]).then_inc(kept_landed[n], 16)

            def stream(ps_index):
                base = ps_index * TILES
                for it in rounds(sp, 2, 2 if ps_index == 0 else 0):
                    for s, (k, h) in enumerate(streamed):
                        if ps_index == 0 and (it, s) in kept_before:
                            load_kept([kept_before[it, s]])
                        before = s - RING
                        k0, h0 = streamed[before]
                        count = 2 * k0 + h0 + 1 - (2 * SPAN if before < 0 else 0)
                        if not (ps_index == 0 and isinstance(it, int) and it == 0 and before < 0):
                            sp.wait_ge(aL_ready, it * (2 * SPAN) + (base + count))
                        sp.dma_start(raw[:, s % RING, :], adjT_tiles[it * SPAN + k, h]).then_inc(tile_landed[s % RING], 16)

            kept_before = {(0, 2): 1, (0, len(streamed) // 2): 2, (1, 2): 3}
            load_kept([0])
            sp.dma_start(par[:], early).then_inc(par_landed, 16)
            for q in range(4):
                stream(q)
            sp.wait_ge(aL_ready, 4 * TILES)
            for r in range(2):
                sp.dma_start(rowbuf[:, r, :], adj_rows[r]).then_inc(row_landed[r], 16)
            with sp.Fori(1, NSB) as sbi:
                for r in range(2):
                    sp.wait_ge(m_ready, sbi * (2 * NCH) + (r + 1 - 2) * NCH)
                    sp.dma_start(rowbuf[:, r, :], adj_rows[sbi * 2 + r]).then_inc(row_landed[r], 16)
            sp.wait_ge(m_ready, NB * NCH)
            sp.wait_ge(pv_done, NSB * NBATCH)
            sp.dma_start(lpar[:], late).then_inc(late_landed, 16)
            load_kept(range(NKEPT))
            stream(4)
            stream(5)
            out_blocks = out.rearrange("(b q) d -> q b d", q=D)
            for c in range(BK):
                sp.wait_ge(x_ready, 3 * BK + c + 1)
                sp.dma_start(out_blocks[:, c * BPB:(c + 1) * BPB, :],
                             chunk(xrow, c).rearrange("p (b d) -> p b d", d=D)).then_inc(out_written, 16)
            sp.wait_ge(out_written, 16 * BK)

        @block.gpsimd
        def _(pool):
            def stage(pass_index, split, beside=None):
                for it in rounds(pool, BK, 1 if pass_index == 0 else 0):
                    wait_alone(pool, yL_ready, it + (split * BK + 1))
                    for r in range(BPB):
                        b = it * BPB + r
                        if not (pass_index == 0 and isinstance(it, int) and it == 0 and r < 2):
                            pool.wait_ge(tile_used, it * (2 * BPB) + (pass_index * TILES + 2 * r - 2))
                        pool.tensor_copy(wH[:, r % 2, :], yH[:, bass.ts(b, D)].bitcast(F32))
                        pool.tensor_copy(wL[:, r % 2, :], yL[:, bass.ts(b, D)].bitcast(F32)).then_inc(w_ready, 1)
                    if beside is not None:
                        beside(it)

            for q in range(4):
                stage(q, q)

            def stage_unit(rb, r, nth):
                if nth is not None:
                    pool.wait_ge(s_ready, nth)
                if not (isinstance(rb, int) and rb == 0):
                    wait_alone(pool, bw_ready, rb)
                c = bass.ts(rb, D)
                pool.tensor_tensor(tmp, unitH[:, c].bitcast(F32), unitL[:, c].bitcast(F32), ALU.add).then_inc(bw_step, 1)
                wait_alone(pool, bw_step, rb * 3 + 1)
                pool.tensor_scalar(tmp, tmp, p("beta"), 0.0, ALU.mult, ALU.add).then_inc(bw_step, 1)
                wait_alone(pool, bw_step, rb * 3 + 2)
                pool.tensor_copy(wH[:, r, :], tmp).then_inc(bw_step, 1)
                wait_alone(pool, bw_step, rb * 3 + 3)
                pool.tensor_tensor(wL[:, r, :], tmp, wH[:, r, :].bitcast(F32), ALU.subtract).then_inc(bw_ready, 1)

            def mask_bias(rb, r):
                for h in range(2):
                    wait_alone(pool, deg_done, rb * 2 + h + 1)
                    t = rowbuf[:, r, h * HALF:(h + 1) * HALF]
                    pool.tensor_scalar(t, t, -1.0, MASK, ALU.add, ALU.mult).then_inc(bias_ready, 1)

            mask_bias(0, 0)
            pool.wait_ge(umax_ready, 1)
            pool.partition_all_reduce(umax[:, 1:2], umax[:, 0:1], D, RMAX).then_inc(umax_all, 1)
            for c in range(BK):
                pool.wait_ge(unit_ready, c + 1)
                for b in range(c * BPB, (c + 1) * BPB):
                    t = xrow[:, b * D:(b + 1) * D]
                    ins = pool.tensor_scalar(t, t, mean[:, b:b + 1], rstd[:, b:b + 1], ALU.subtract, ALU.mult)
                ins.then_inc(x_ready, 1)
                if c == 2:
                    pool.wait_ge(tile_used, 4 * TILES)
                    pool.wait_ge(unitL_ready, 1)
                    stage_unit(0, 0, None)
            stage_unit(1, 1, None)
            mask_bias(1, 1)
            pool.wait_ge(unitL_ready, BK)
            with pool.Fori(1, NSB) as sbi:
                for r in range(2):
                    stage_unit(sbi * 2 + r, r, sbi * (2 * NCH) + (r + 1 - 2) * NCH)
                    mask_bias(sbi * 2 + r, r)
            stage(4, 5)

            def residual(c):
                wait_alone(pool, self_ready, c + 1)
                t = xrow[:, bass.ts(c, BANK)]
                pool.tensor_tensor(t, t, xT[:, bass.ts(c, BANK)], ALU.add).then_inc(sum_ready, 1)

            stage(5, 6, beside=residual)

        @block.scalar
        def _(act):
            def split_high(pass_index):
                base = pass_index * TILES
                phase = pass_index if pass_index < 4 else pass_index - 4
                for it in rounds(act, 2, 2):
                    s = 0
                    for k in range(SPAN):
                        for h in range(2):
                            tile = 2 * SPAN * it + 2 * k + h
                            if k in KEPT_AT:
                                n = 2 * it + KEPT_AT.index(k)
                                src = kept[:, n, h * HALF:(h + 1) * HALF]
                                if phase == 0 and h == 0:
                                    act.wait_ge(kept_landed[n], 16 * (1 if pass_index < 4 else 2))
                            else:
                                src = raw[:, s % RING, :]
                                uses = 2 * len(range(s % RING, 2 * (SPAN - 2), RING))
                                nth = pass_index * uses + it * (uses // 2) + s // RING + 1
                                act.wait_ge(tile_landed[s % RING], 16 * nth)
                                s += 1
                            if base + tile >= 2:
                                act.wait_ge(aH_used, base + tile - 1)
                                act.wait_ge(aL_ready, base + tile - 1)
                            nc.scalar.activation(aH[:, h, :], src, ACT.Copy).then_inc(aH_ready, 1)

            def high(c, src, split):
                nc.scalar.activation(chunk(yH, c), src, ACT.Copy).then_inc(yH_ready, 1)

            def project(tq, pass_index, func):
                for step in range(BK + 2):
                    b = step
                    if b < BK:
                        wait_bank(act, pass_index, b)
                        if tq * BK + b >= 3:
                            act.wait_ge(proj_done, tq * BK + b - 2)
                        nc.scalar.activation(gT0[b % 3], ps[:, b, :], func).then_inc(g_ready, 1)
                    c = step - 2
                    if c >= 0 and tq < 3:
                        if tq == 1:
                            act.wait_ge(proj_done, tq * BK + c + 1)
                            high(c, ps[:, c, :], tq + 1)
                        else:
                            zn = (tq // 2) * BK + c
                            act.wait_ge(z_ready, zn + 1)
                            high(c, z0[c % 2], tq + 1)

            def root(n):
                w = 2 * NB if n == 0 else NB
                act.wait_ge(var_ready, n + 1)
                nc.scalar.activation(s2[:, 0:w], s1[:, 0:w], ACT.Sqrt).then_inc(root_ready, 1)

            for c in range(BK):
                if c % HBK == 0:
                    act.wait_ge(x_landed[c // HBK], 16)
                high(c, chunk(xrow, c), 0)
            for q in range(3):
                split_high(q)
                project(q, q, ACT.Relu if q == 1 else ACT.Copy)
            split_high(3)
            project(3, 3, ACT.Copy)
            def degrees(rb, r, h, sbi):
                if h == 0:
                    act.wait_ge(row_landed[r], sbi * 16 + 16)
                t = rowbuf[:, r, h * HALF:(h + 1) * HALF]
                nc.scalar.activation(t, t, ACT.Copy, accum_out=degp[:, bass.ds(rb, 1), h]).then_inc(deg_done, 1)

            def exponent(rb, slot, c):
                if c == 0:
                    act.wait_ge(max_ready, rb + 1)
                t = kept[:, slot, c * CH:(c + 1) * CH]
                nc.scalar.activation(t, t, ACT.Exp, bias=nmax[:, bass.ds(rb, 1)],
                                     accum_out=psums[:, bass.ds(rb, 1), c]).then_inc(exp_done, 1)

            def turned_high(sbi, k):
                n = sbi * NBATCH + k
                act.wait_ge(pt_ready, n + 1)
                if not (isinstance(sbi, int) and sbi == 0 and k < 2):
                    act.wait_ge(pv_done, n - 1)
                nc.scalar.activation(ptH[:, k % 2, :], ps[:, PT_BANKS[k % 2], :], ACT.Copy).then_inc(ptH_ready, 1)

            def o_copy(sbi):
                act.wait_ge(pv_done, sbi * NBATCH + NBATCH)
                nc.scalar.activation(oT[:], ps[:, O_BANK, 0:2 * D], ACT.Copy).then_inc(o_copied, 1)

            def super_block(sbi, parity, more, before):
                nxt = sbi + 1
                first_r0, first_r1 = 2 * NCH + 1 - LEAD, 4 * NCH + 1 - LEAD
                for k in range(NBATCH):
                    if k == 0 and before:
                        o_copy(sbi - 1)
                    if k not in HIGH_BY_DVE:
                        turned_high(sbi, k)
                    if k + NBATCH - first_r1 < NCH and before:
                        exponent(sbi * 2 + 1, 2 * parity + 1, k + NBATCH - first_r1)
                    if first_r0 <= k < first_r0 + NCH and more >= 1:
                        exponent(nxt * 2, 2 * (1 - parity), k - first_r0)
                    if k >= first_r1 and more >= 1:
                        exponent(nxt * 2 + 1, 2 * (1 - parity) + 1, k - first_r1)
                    if k in (1, 3) and more >= 1:
                        degrees(nxt * 2 + 1, 1, k // 2, nxt)
                    if k in (9, 11) and more == 2:
                        degrees((nxt + 1) * 2, 0, (k - 9) // 2, nxt + 1)

            for h in range(2):
                degrees(0, 0, h, 0)
            root(0)
            for c in range(BK):
                act.wait_ge(unitT_done, c + 1)
                nc.scalar.activation(chunk(unitH, c), ps[:, c, :], ACT.Copy).then_inc(unitH_ready, 1)
            act.wait_ge(unormT_done, 1)
            nc.scalar.activation(uT, ps[0:NB, OT_BANK, 0:D], ACT.Copy).then_inc(uT_ready, 1)
            for c in range(BK):
                act.wait_ge(uspread_done, c + 1)
                nc.scalar.activation(chunk(xT, c), ps[:, HBK + c % HBK, :], ACT.Copy).then_inc(urow_ready, 1)
            for c in range(BK):
                act.wait_ge(x_ready, c + 1)
                high(c, chunk(xrow, c), 4)
                if c in (0, 2):
                    degrees(1, 1, c // 2, 0)
            for r in range(2):
                for c in range(NCH):
                    exponent(r, r, c)
            for h in range(2):
                degrees(2, 0, h, 1)
            super_block(0, 0, 2, False)
            with act.Fori(0, (NSB - 4) // 2) as it:
                super_block(it * 2 + 1, 1, 2, True)
                super_block(it * 2 + 2, 0, 2, True)
            super_block(NSB - 3, 1, 2, True)
            super_block(NSB - 2, 0, 1, True)
            super_block(NSB - 1, 1, 0, True)
            o_copy(NSB - 1)
            root(1)

            def split_and_turn(ln, split):
                for step in range(BK + 1):
                    if step < BK:
                        act.wait_ge(x_ready, ln * BK + step + 1)
                        high(step, chunk(xrow, step), split)
                    c = step - 1
                    if c >= 0:
                        act.wait_ge(xT_done, (ln - 1) * BK + c + 1)
                        nc.scalar.activation(chunk(xT, c), ps[:, c, :], ACT.Copy).then_inc(xT_ready, 1)

            split_and_turn(1, 5)
            split_high(4)
            for c in range(BK):
                wait_bank(act, 4, c)
                nc.scalar.activation(chunk(xrow, c), ps[:, c, :], ACT.Copy).then_inc(g_ready, 1)

            def message(c):
                act.wait_ge(msg_done, c + 1)
                nc.scalar.activation(msg_s[c % 2], ps[:, 0, :], ACT.Relu, bias=p("bm")).then_inc(msg_ready, 1)

            message(0)
            for c in range(BK):
                if c + 1 < BK:
                    message(c + 1)
                act.wait_ge(r_done, c + 1)
                nc.scalar.activation(r_s[c % 2], ps[:, 1, :], ACT.Sigmoid, bias=bsum[:, 0:1]).then_inc(r_ready, 1)
                act.wait_ge(zg_done, c + 1)
                nc.scalar.activation(z_s[c % 2], ps[:, 2, :], ACT.Sigmoid, bias=bsum[:, 1:2]).then_inc(zg_ready, 1)
                act.wait_ge(narg_ready, c + 1)
                nc.scalar.activation(n_s[c % 2], chunk(xrow, c), ACT.Tanh, bias=p("bih", 2, 3)).then_inc(n_ready, 1)
            root(2)

            split_and_turn(2, 6)
            for c in range(BK):
                act.wait_ge(self_done, c + 1)
                nc.scalar.activation(chunk(xT, c), ps[:, c, :], ACT.Copy).then_inc(self_ready, 1)
            split_high(5)
            act.wait_ge(sum_ready, BK)
            for b in range(BK):
                wait_bank(act, 5, b)
                nc.scalar.activation(chunk(xT, b), ps[:, b, :], ACT.Copy).then_inc(g_ready, 1)
            root(3)

        @block.vector
        def _(dve):
            chain = [0]

            def link(ins):
                chain[0] += 1
                ins.then_inc(dve_step, 1)
                dve.wait_ge(dve_step, chain[0])

            def split_low(pass_index):
                base = pass_index * TILES
                for it in rounds(dve, 2, 2):
                    s = 0
                    for k in range(SPAN):
                        for h in range(2):
                            if k in KEPT_AT:
                                src = kept[:, 2 * it + KEPT_AT.index(k), h * HALF:(h + 1) * HALF]
                            else:
                                src = raw[:, s % RING, :]
                                s += 1
                            tile = 2 * SPAN * it + 2 * k + h
                            if base + tile >= 2:
                                dve.wait_ge(tile_used, base + tile - 1)
                            dve.wait_ge(aH_ready, base + tile + 1)
                            dve.tensor_tensor(aL[:, h, :], src, aH[:, h, :].bitcast(F32), ALU.subtract).then_inc(aL_ready, 1)

            def low(c, src, split):
                dve.wait_ge(yH_ready, split * BK + c + 1)
                dve.tensor_tensor(chunk(yL, c), src, chunk(yH, c).bitcast(F32), ALU.subtract).then_inc(yL_ready, 1)

            def project(tq):
                for step in range(BK + 1):
                    c = step
                    if c < BK and tq != 1:
                        zn = (tq // 2) * BK + c
                        dve.wait_ge(proj_done, tq * BK + c + 1)
                        if zn >= 2:
                            dve.wait_ge(yL_ready, (tq + 1) * BK + c - 1 if c >= 2 else tq * BK + BK)
                        filt = p("f1" if tq == 0 else "f2", c * BPB, (c + 1) * BPB)
                        dve.tensor_tensor(z0[c % 2].rearrange("p (b d) -> p b d", d=D),
                                          ps[:, c, :].rearrange("p (b d) -> p b d", d=D),
                                          filt.unsqueeze(2).to_broadcast([D, BPB, D]), ALU.mult).then_inc(z_ready, 1)
                    c = step - 1
                    if c >= 0:
                        if tq == 1:
                            low(c, ps[:, c, :], tq + 1)
                        else:
                            dve.wait_ge(z_ready, (tq // 2) * BK + c + 1)
                            low(c, z0[c % 2], tq + 1)

            def bank_stats(c, own, value):
                dve.wait_ge(own, value)
                for b in range(c * BPB, (c + 1) * BPB):
                    ins = dve.bn_stats(stats[:, b:b + 1, :], xrow[:, b * D:(b + 1) * D])
                ins.then_inc(stats_ready, 1)

            def row_scales(nroot, value):
                w = 2 * NB if nroot == 0 else NB
                dve.wait_ge(stats_ready, value)
                mean_e, mean_o = stats[:, :, 1], stats[:, :, 4]
                m2_e, m2_o = stats[:, :, 2], stats[:, :, 5]
                v, d = s1[:, 0:NB], s2[:, 0:NB]
                dve.tensor_tensor(v, m2_e, m2_o, ALU.add)
                dve.tensor_tensor(s3[:, 0:NB], mean_e, mean_o, ALU.add)
                link(dve.tensor_tensor(d, mean_e, mean_o, ALU.subtract))
                dve.tensor_scalar(mean[:], s3[:, 0:NB], 0.5, None, ALU.mult)
                link(dve.scalar_tensor_tensor(out=d, in0=d, scalar=0.25, in1=d, op0=ALU.mult, op1=ALU.mult))
                link(dve.scalar_tensor_tensor(out=v, in0=v, scalar=1.0 / D, in1=d, op0=ALU.mult, op1=ALU.add))
                if nroot == 0:
                    link(dve.tensor_scalar(s1[:, NB:w], v, float(D), TINY, ALU.mult, ALU.max))
                dve.tensor_scalar(v, v, LN_EPS, None, ALU.add).then_inc(var_ready, 1)
                a, r, q = s1[:, 0:w], s2[:, 0:w], s3[:, 0:w]
                dve.wait_ge(root_ready, nroot + 1)
                link(dve.reciprocal(q, r))
                link(dve.tensor_tensor(q, q, a, ALU.mult))
                link(dve.tensor_tensor(q, q, r, ALU.add))
                link(dve.tensor_scalar(r, q, 0.5, None, ALU.mult))
                if nroot == 0:
                    link(dve.reciprocal(q, r))
                    link(dve.tensor_tensor(unorm[:], s2[:, 0:NB], s3[:, NB:w], ALU.mult))
                    dve.tensor_reduce(umax[:, 0:1], unorm[:], AX.X, ALU.max).then_inc(umax_ready, 1)
                    dve.tensor_scalar(epsu[:], unorm[:], COS_EPS, None, ALU.mult).then_inc(unorm_ready, 1)
                    link(dve.tensor_copy(rstd[:], s3[:, 0:NB]))
                else:
                    link(dve.reciprocal(rstd[:], r))

            def normalise(c):
                for b in range(c * BPB, (c + 1) * BPB):
                    t = xrow[:, b * D:(b + 1) * D]
                    ins = dve.tensor_scalar(t, t, mean[:, b:b + 1], rstd[:, b:b + 1], ALU.subtract, ALU.mult)
                ins.then_inc(x_ready, 1)

            for c in range(BK):
                low(c, chunk(xrow, c), 0)
            for q in range(3):
                split_low(q)
                project(q)
            split_low(3)
            for c in range(BK):
                dve.wait_ge(proj_done, 3 * BK + c + 1)
                dve.tensor_tensor(chunk(xrow, c), ps[:, c, :], chunk(xrow, c), ALU.add).then_inc(t_ready, 1)
                if c >= 1:
                    bank_stats(c - 1, t_ready, c)
            bank_stats(BK - 1, t_ready, BK)
            row_scales(0, BK)

            for step in range(BK + 2):
                if step < BK:
                    for b in range(step * BPB, (step + 1) * BPB):
                        ins = dve.tensor_scalar(kept[:, 3, b * D:(b + 1) * D], xrow[:, b * D:(b + 1) * D],
                                                mean[:, b:b + 1], s3[:, NB + b:NB + b + 1], ALU.subtract, ALU.mult)
                    ins.then_inc(unit_ready, 1)
                c = step - 2
                if c >= 0:
                    dve.wait_ge(unitH_ready, c + 1)
                    dve.tensor_tensor(chunk(unitL, c), ps[:, c, :], chunk(unitH, c).bitcast(F32), ALU.subtract).then_inc(unitL_ready, 1)
            dve.wait_ge(umax_all, 1)
            link(dve.tensor_scalar(flag[:], umax[:, 1:2], PRODUCT_SAFE, None, ALU.is_gt))
            small_norms = dve.value_load(flag[0:1, 0:1], min_val=0, max_val=1)

            def mask(rb, r, slot, c):
                n = rb * NCH + c
                with dve.If(small_norms > 0):
                    dve.wait_ge(s_ready, n + 1)
                    dve.wait_ge(urow_ready, BK)
                    corr = kept[:, slot, c * CH:(c + 1) * CH]
                    dve.tensor_scalar(corr, xT[:, c * CH:(c + 1) * CH], epsu[:, bass.ds(rb, 1)], 1.0, ALU.mult, ALU.add)
                    dve.drain()
                    dve.reciprocal(corr, corr)
                    dve.drain()
                    dve.tensor_tensor(S2[c % 2], S2[c % 2], corr, ALU.mult)
                    dve.drain()
                wait_alone(dve, s_ready, n + 1)
                if c in (0, NCH // 2):
                    wait_alone(dve, bias_ready, rb * 2 + c // (NCH // 2) + 1)
                dve.tensor_tensor_reduce(kept[:, slot, c * CH:(c + 1) * CH], S2[c % 2], rowbuf[:, r, c * CH:(c + 1) * CH],
                                         1.0, LOWEST, ALU.add, ALU.max, cmax[:, r, c:c + 1]).then_inc(m_ready, 1)
                if c == NCH - 1:
                    dve.wait_ge(m_ready, n + 1)
                    dve.tensor_reduce(nmax[:, bass.ds(rb, 1)], cmax[:, r, :], AX.X, ALU.max,
                                      negate=True).then_inc(max_ready, 1)

            def turned_low(sbi, k):
                if k in HIGH_BY_DVE:
                    own = HIGH_BY_DVE.index(k)
                    dve.wait_ge(pt_ready, sbi * NBATCH + k + 1)
                    if not (isinstance(sbi, int) and sbi == 0 and k < 2):
                        dve.wait_ge(pv_done, sbi * NBATCH + (k - 1))
                    dve.tensor_copy(ptH[:, k % 2, :], ps[:, PT_BANKS[k % 2], :]).then_inc(ptH_own, 1)
                    dve.wait_ge(ptH_own, sbi * len(HIGH_BY_DVE) + (own + 1))
                else:
                    dve.wait_ge(ptH_ready, sbi * len(BY_ACT) + (BY_ACT.index(k) + 1))
                dve.tensor_tensor(ptL[:, k % 2, :], ps[:, PT_BANKS[k % 2], :], ptH[:, k % 2, :].bitcast(F32),
                                  ALU.subtract).then_inc(ptL_ready, 1)

            def o_rows(sbi):
                rows = bass.ds(sbi * 2, 2)
                dve.wait_ge(o_turned, sbi + 1)
                dve.tensor_reduce(rsum[:], psums[:, rows, :], AX.X, ALU.add).then_inc(o_step, 1)
                dve.wait_ge(o_step, sbi * 2 + 1)
                dve.reciprocal(rsum[:], rsum[:]).then_inc(o_step, 1)
                dve.wait_ge(o_step, sbi * 2 + 2)
                for r in range(2):
                    b = sbi * 2 + r
                    t = xrow[:, bass.ts(b, D)]
                    ins = dve.scalar_tensor_tensor(out=t, in0=ps[:, OT_BANK, r * D:(r + 1) * D], scalar=rsum[:, r:r + 1],
                                                   in1=t, op0=ALU.mult, op1=ALU.add)
                ins.then_inc(o_done, 1)
                wait_alone(dve, o_done, sbi + 1)
                for r in range(2):
                    b = sbi * 2 + r
                    dve.bn_stats(stats[:, bass.ds(b, 1), :], xrow[:, bass.ts(b, D)]).then_inc(stats_ready, 1)

            def mask_chunk(sbi, parity, m):
                r, c = divmod(m, NCH)
                mask(sbi * 2 + r, r, 2 * parity + r, c)

            def super_block(sbi, parity, more, before):
                for k in range(NBATCH):
                    m = (k + LEAD - 2) // 2
                    if k % 2 == 0 and m < 2 * NCH and more >= 1:
                        mask_chunk(sbi + 1, 1 - parity, m)
                    if k % 2 == 0 and m >= 2 * NCH and more == 2:
                        mask_chunk(sbi + 2, parity, m - 2 * NCH)
                    turned_low(sbi, k)
                    if k == 3 and before:
                        o_rows(sbi - 1)

            for m in range(2 * NCH):
                mask_chunk(0, 0, m)
                if m >= NCH:
                    for c in range(2 * (m - NCH), 2 * (m - NCH) + 2):
                        low(c, chunk(xrow, c), 4)
            mask_chunk(1, 1, 0)
            super_block(0, 0, 2, False)
            with dve.Fori(0, (NSB - 4) // 2) as it:
                super_block(it * 2 + 1, 1, 2, True)
                super_block(it * 2 + 2, 0, 2, True)
            super_block(NSB - 3, 1, 2, True)
            super_block(NSB - 2, 0, 1, True)
            super_block(NSB - 1, 1, 0, True)
            o_rows(NSB - 1)
            link(dve.tensor_reduce(rdeg[:], degp[:], AX.X, ALU.add))
            link(dve.tensor_scalar(rdeg[:], rdeg[:], 1.0, None, ALU.max))
            link(dve.reciprocal(rdeg[:], rdeg[:]))
            dve.tensor_tensor(bsum[:], p("bih", 0, 2), p("bhh", 0, 2), ALU.add)
            row_scales(1, BK + NB)

            def normalise_and_split(split):
                for step in range(BK + 1):
                    if step < BK:
                        normalise(step)
                    if step >= 1:
                        low(step - 1, chunk(xrow, step - 1), split)

            normalise_and_split(5)
            split_low(4)

            def gru_rows(c):
                dve.wait_ge(gruT_done, c + 1)
                dve.tensor_copy(chunk(xrow, c), ps[:, 5, :]).then_inc(t_ready, 1)

            for c in range(BK):
                h, t, ng, zg = chunk(xT, c), g_s[c % 2], n_s[c % 2], z_s[c % 2]
                narg = chunk(xrow, c)
                dve.wait_ge(r_ready, c + 1)
                dve.wait_ge(hn_done, c + 1)
                dve.scalar_tensor_tensor(out=narg, in0=ps[:, 4, :], scalar=p("bhh", 2, 3), in1=r_s[c % 2],
                                         op0=ALU.add, op1=ALU.mult).then_inc(hn_used, 1)
                dve.wait_ge(hn_used, c + 1)
                dve.wait_ge(in_done, c + 1)
                dve.tensor_tensor(narg, narg, ps[:, 3, :], ALU.add).then_inc(narg_ready, 1)
                if c >= 1:
                    gru_rows(c - 1)
                dve.wait_ge(n_ready, c + 1)
                dve.tensor_tensor(t, h, ng, ALU.subtract).then_inc(gru_step, 1)
                dve.wait_ge(gru_step, 3 * c + 1)
                dve.wait_ge(zg_ready, c + 1)
                dve.tensor_tensor(t, t, zg, ALU.mult).then_inc(gru_step, 1)
                dve.wait_ge(gru_step, 3 * c + 2)
                dve.tensor_tensor(t, t, ng, ALU.add).then_inc(gru_step, 1)
                dve.wait_ge(gru_step, 3 * c + 3)
                dve.tensor_tensor(t, t, h, ALU.add).then_inc(gru_ready, 1)
                if c >= 1:
                    bank_stats(c - 1, t_ready, BK + c)
            gru_rows(BK - 1)
            bank_stats(BK - 1, t_ready, 2 * BK)
            row_scales(2, 2 * BK + NB)

            normalise_and_split(6)
            split_low(5)
            dve.wait_ge(sum_ready, BK)
            for c in range(BK):
                dve.wait_ge(proj_done, 4 * BK + c + 1)
                for i in range(BPB):
                    b = c * BPB + i
                    t = xrow[:, b * D:(b + 1) * D]
                    ins = dve.scalar_tensor_tensor(out=t, in0=ps[:, c, i * D:(i + 1) * D], scalar=rdeg[:, b:b + 1],
                                                   in1=t, op0=ALU.mult, op1=ALU.add)
                ins.then_inc(t_ready, 1)
                if c >= 1:
                    bank_stats(c - 1, t_ready, 2 * BK + c)
            bank_stats(BK - 1, t_ready, 3 * BK)
            row_scales(3, 3 * BK + NB)
            for c in range(BK):
                normalise(c)

        @block.tensor
        def _(pe):
            def multiply(pass_index, read=None, value=0):
                def tiles(it, first, last):
                    for r in range(2):
                        for h in range(2):
                            tile = 4 * it + (pass_index * TILES + 2 * r + h)
                            banks = [ps[:, h * HBK + j, :] for j in range(HBK)]
                            cols = [slice(j * BANK, (j + 1) * BANK) for j in range(HBK)]
                            if h == 0:
                                pe.wait_ge(w_ready, 2 * it + (pass_index * NB + r + 1))
                            if first and r == 0 and read is not None:
                                pe.wait_ge(read, value - (HBK if h == 0 else 0))
                            pe.wait_ge(aH_ready, tile + 1)
                            for b, c in zip(banks, cols):
                                pe.matmul(b, wH[:, r, :], aH[:, h, c], start=first and r == 0, stop=False)
                            for b, c in zip(banks, cols):
                                ins = pe.matmul(b, wL[:, r, :], aH[:, h, c], start=False, stop=False)
                            ins.then_inc(aH_used, 1)
                            pe.wait_ge(aL_ready, tile + 1)
                            done = last and r == 1
                            for b, c in zip(banks, cols):
                                ins = pe.matmul(b, wH[:, r, :], aL[:, h, c], start=False, stop=done)
                                if done and c.stop < HALF:
                                    ins.then_inc(bank_done, 1)
                            ins.then_inc(tile_used, 1)
                tiles(0, True, False)
                with pe.Fori(1, NB // 2 - 1) as it:
                    tiles(it, False, False)
                tiles(NB // 2 - 1, False, True)

            def project(tq, weights, turned):
                for b in range(BK):
                    pe.wait_ge(g_ready, (tq if tq < 4 else 5) * BK + b + 1)
                    for i in range(BPB):
                        o, t = ps[:, b, i * D:(i + 1) * D], turned[b % len(turned)][:, i * D:(i + 1) * D]
                        if weights is None:
                            ins = pe.transpose(o, t, ident)
                        else:
                            ins = pe.matmul(o, t, weights, start=True, stop=True)
                    ins.then_inc(proj_done, 1)

            def turn(src, ready, base, done):
                for c in range(BK):
                    pe.wait_ge(ready, base + c + 1)
                    for i in range(BPB):
                        ins = pe.transpose(ps[:, c, i * D:(i + 1) * D], src[:, c * BANK + i * D:c * BANK + (i + 1) * D], ident)
                    ins.then_inc(done, 1)

            for q in range(4):
                multiply(q, *[(), (z_ready, BK), (yL_ready, 3 * BK), (z_ready, 2 * BK)][q])
                if q == 0:
                    pe.wait_ge(par_landed, 16)
                project(q, [p("W1"), p("W2"), None, None][q], gT0)

            turn(kept[:, 3, :], unit_ready, 0, unitT_done)

            def spread_norms():
                pe.wait_ge(unorm_ready, 1)
                pe.wait_ge(unitL_ready, BK)
                pe.transpose(ps[0:NB, OT_BANK, 0:D], unorm[:], ident).then_inc(unormT_done, 1)
                pe.wait_ge(uT_ready, 1)
                for c in range(BK):
                    if c >= HBK:
                        pe.wait_ge(urow_ready, c - HBK + 1)
                    for i in range(BPB):
                        b = c * BPB + i
                        ins = pe.matmul(ps[:, HBK + c % HBK, i * D:(i + 1) * D], ident[0:NB, b:b + 1].to_broadcast([NB, D]),
                                        uT, start=True, stop=True)
                    ins.then_inc(uspread_done, 1)

            def scores(sbi, q):
                m, j = divmod(q, CH // BANK)
                r, c = divmod(m, NCH)
                if j == 0:
                    if c == 0:
                        pe.wait_ge(bw_ready, sbi * 2 + (r + 1))
                    if not (isinstance(sbi, int) and sbi == 0 and m < 2):
                        pe.wait_ge(m_ready, sbi * (2 * NCH) + (m - 1))
                o = ps[:, S_BANKS[c % 2] + j, :]
                col = slice(c * CH + j * BANK, c * CH + (j + 1) * BANK)
                pe.matmul(o, wH[:, r, :], unitH[:, col], start=True, stop=False)
                pe.matmul(o, wH[:, r, :], unitL[:, col], start=False, stop=False)
                ins = pe.matmul(o, wL[:, r, :], unitH[:, col], start=False, stop=True)
                if j == CH // BANK - 1:
                    ins.then_inc(s_ready, 1)

            def turn_batch(sbi, parity, k, first):
                n = sbi * NBATCH + k
                if k % (NBATCH // NCH) == 0:
                    pe.wait_ge(exp_done, sbi * (2 * NCH) + (NCH + k // (NBATCH // NCH) + 1))
                if not first:
                    pe.wait_ge(ptL_ready, n - 1)
                for a in range(2):
                    for r in range(2):
                        j = 2 * k + a
                        ins = pe.transpose(ps[:, PT_BANKS[k % 2], (2 * a + r) * D:(2 * a + r + 1) * D],
                                           kept[:, 2 * parity + r, j * D:(j + 1) * D], ident)
                ins.then_inc(pt_ready, 1)

            def sum_batch(sbi, k, before):
                n = sbi * NBATCH + k
                if k == 0 and before:
                    pe.wait_ge(o_copied, sbi)
                pe.wait_ge(ptL_ready, n + 1)
                o = ps[:, O_BANK, 0:2 * D]
                for a in range(2):
                    j = 2 * k + a
                    jc, cols = slice(j * D, (j + 1) * D), slice(a * 2 * D, (a + 1) * 2 * D)
                    pe.matmul(o, yH[:, jc], ptH[:, k % 2, cols], start=(j == 0), stop=False)
                    pe.matmul(o, yH[:, jc], ptL[:, k % 2, cols], start=False, stop=False)
                    ins = pe.matmul(o, yL[:, jc], ptH[:, k % 2, cols], start=False, stop=(j == NB - 1))
                ins.then_inc(pv_done, 1)

            def turn_sums(sbi, first):
                pe.wait_ge(o_copied, sbi + 1)
                if not first:
                    pe.wait_ge(o_done, sbi)
                for r in range(2):
                    ins = pe.transpose(ps[:, OT_BANK, r * D:(r + 1) * D], oT[:, r * D:(r + 1) * D], ident)
                ins.then_inc(o_turned, 1)

            def super_block(sbi, parity, more, before, second=False):
                for k in range(NBATCH):
                    turn_batch(sbi, parity, k, not before and k < 2)
                    if k < NBATCH - LEAD and more >= 1:
                        scores(sbi + 1, k + LEAD)
                    if k >= NBATCH - LEAD and more == 2:
                        scores(sbi + 2, k - NBATCH + LEAD)
                    if k >= 1:
                        sum_batch(sbi, k - 1, before)
                    if k == 2 and before:
                        turn_sums(sbi - 1, second)
                sum_batch(sbi, NBATCH - 1, before)

            for q in range(NBATCH):
                if q < BK:
                    pe.wait_ge(unitL_ready, q + 1)
                if q == LEAD:
                    spread_norms()
                scores(0, q)
            for q in range(LEAD):
                if q == 0:
                    pe.wait_ge(urow_ready, BK)
                scores(1, q)
            super_block(0, 0, 2, False)
            super_block(1, 1, 2, True, True)
            super_block(2, 0, 2, True)
            with pe.Fori(1, (NSB - 4) // 2) as it:
                super_block(it * 2 + 1, 1, 2, True)
                super_block(it * 2 + 2, 0, 2, True)
            super_block(NSB - 3, 1, 2, True)
            super_block(NSB - 2, 0, 1, True)
            super_block(NSB - 1, 1, 0, True)
            turn_sums(NSB - 1, False)

            pe.wait_ge(o_done, NSB)
            turn(xrow, x_ready, BK, xT_done)
            multiply(4, xT_ready, BK)
            pe.wait_ge(late_landed, 16)
            pe.wait_ge(g_ready, 5 * BK)

            def message(c):
                if c >= 1:
                    pe.wait_ge(msg_ready, c)
                pe.matmul(ps[:, 0, :], p("WmT"), chunk(xrow, c), start=True, stop=True).then_inc(msg_done, 1)

            def gru_turn(c):
                pe.wait_ge(gru_ready, c + 1)
                if c >= 1:
                    pe.wait_ge(t_ready, BK + c)
                for i in range(BPB):
                    ins = pe.transpose(ps[:, 5, i * D:(i + 1) * D], g_s[c % 2][:, i * D:(i + 1) * D], ident)
                ins.then_inc(gruT_done, 1)

            def gate(bank, wi, wh, c):
                pe.matmul(ps[:, bank, :], p("WhhT")[:, wh], chunk(xT, c), start=True, stop=False)
                return pe.matmul(ps[:, bank, :], p("WihT")[:, wi], msg_s[c % 2], start=False, stop=True)

            R, Z, NG = (slice(i * D, (i + 1) * D) for i in range(3))
            message(0)
            for c in range(BK):
                if c + 1 < BK:
                    message(c + 1)
                pe.wait_ge(msg_ready, c + 1)
                if c >= 1:
                    pe.wait_ge(r_ready, c)
                gate(1, R, R, c).then_inc(r_done, 1)
                if c >= 1:
                    pe.wait_ge(zg_ready, c)
                gate(2, Z, Z, c).then_inc(zg_done, 1)
                if c >= 1:
                    pe.wait_ge(hn_used, c)
                pe.matmul(ps[:, 4, :], p("WhhT")[:, NG], chunk(xT, c), start=True, stop=True).then_inc(hn_done, 1)
                if c >= 1:
                    pe.wait_ge(narg_ready, c)
                pe.matmul(ps[:, 3, :], p("WihT")[:, NG], msg_s[c % 2], start=True, stop=True).then_inc(in_done, 1)
                if c >= 1:
                    gru_turn(c - 1)
            gru_turn(BK - 1)

            turn(xrow, x_ready, 2 * BK, xT_done)
            for c in range(BK):
                pe.wait_ge(xT_ready, BK + c + 1)
                for i in range(BPB):
                    ins = pe.matmul(ps[:, c, i * D:(i + 1) * D], chunk(xT, c)[:, i * D:(i + 1) * D], p("Ws"), start=True, stop=True)
                ins.then_inc(self_done, 1)
            multiply(5, self_ready, BK)
            project(4, p("Wn"), [chunk(xT, b) for b in range(BK)])


NAMES = ("x_rows", "adjT", "adj", "early", "late")


def kernel(x, adj, L0_gnn_W1, L0_gnn_f1, L0_gnn_W2, L0_gnn_f2, L1_gnn_beta, L2_gnn_W_msg, L2_gnn_b_msg, L2_gnn_W_ih,
           L2_gnn_W_hh, L2_gnn_b_ih, L2_gnn_b_hh, L3_gnn_W_self, L3_gnn_W_neigh):
    import numpy as np
    import concourse.bacc as bacc
    from concourse.bass_utils import run_bass_kernel_spmd

    x, adj = np.asarray(x), np.asarray(adj)
    N = x.shape[0]
    NB = N // D

    def columns(v, n):
        return np.asarray(v).reshape(n, D).T

    packed = {
        "f1": columns(L0_gnn_f1, NB), "f2": columns(L0_gnn_f2, NB),
        "W1": np.asarray(L0_gnn_W1), "W2": np.asarray(L0_gnn_W2), "WmT": np.asarray(L2_gnn_W_msg).T,
        "WihT": np.asarray(L2_gnn_W_ih).T, "WhhT": np.asarray(L2_gnn_W_hh).T,
        "Ws": np.asarray(L3_gnn_W_self), "Wn": np.asarray(L3_gnn_W_neigh), "ident": np.eye(D, dtype=np.float32),
        "bm": columns(L2_gnn_b_msg, 1), "bih": columns(L2_gnn_b_ih, 3), "bhh": columns(L2_gnn_b_hh, 3),
        "beta": np.broadcast_to(np.asarray(L1_gnn_beta).reshape(1, 1), (D, 1)),
    }
    early, late = (np.ascontiguousarray(np.concatenate([packed[name] for name in names], axis=1)) for names in (EARLY, LATE))
    x_rows = np.ascontiguousarray(x.reshape(NB, D, D).transpose(1, 0, 2).reshape(D, N))
    arrays = {"x_rows": x_rows, "adjT": np.ascontiguousarray(adj.T), "adj": np.ascontiguousarray(adj), "early": early, "late": late}

    nc = bacc.Bacc("TRN2", target_bir_lowering=False, num_devices=1)
    args = [nc.dram_tensor(n, arrays[n].shape, F32, kind="ExternalInput").ap() for n in NAMES]
    out = nc.dram_tensor("out", (N, D), F32, kind="ExternalOutput").ap()
    build(nc, *args, out)
    r = run_bass_kernel_spmd(nc, [arrays], core_ids=[0])
    return r.results[0]["out"]
```

```python
from contextlib import ExitStack

import concourse.bass as bass
from concourse import mybir

ALU = mybir.AluOpType
ACT = mybir.ActivationFunctionType
AX = mybir.AxisListType
F32 = mybir.dt.float32
F32R = mybir.dt.float32r
I32 = mybir.dt.int32
RMAX = bass.bass_isa.ReduceOp.max

D = 128
BANK = 512
BPB = BANK // D
MASK = 1.0e9
COS_EPS = 1e-7
LN_EPS = 1e-5
TINY = 1e-30
PRODUCT_SAFE = 0.7
LOWEST = -3.4028234e38

EARLY = {"f1": None, "f2": None, "W1": D, "W2": D, "ident": D, "bm": 1, "bih": 3, "bhh": 3, "beta": 1}
LATE = {"WmT": D, "WihT": 3 * D, "WhhT": 3 * D, "Ws": D, "Wn": D}


def columns_of(names, NB):
    at, where = 0, {}
    for name, width in names.items():
        where[name] = (at, NB if width is None else width)
        at += where[name][1]
    return where, at


def build(nc, x_rows, adjT, adj, early, late, norms, out):
    N = adj.shape[0]
    NB = N // D
    BK = N // BANK
    HALF = N // 2
    HBK = BK // 2
    SPAN = NB // 2
    KEPT_AT = tuple(range(0, 2 * SPAN, 8))
    NKEPT = 2 * len(KEPT_AT)
    RING = 4
    TILES = 2 * NB
    CH = 1024
    NCH = N // CH
    NSB = NB // 2
    NBATCH = NB // 2
    FIRST, SECOND = (0, 1), (1, 2)
    LEAD = 4
    BY_ACT_LAST = (1, 3, 5, 7)
    SCALE_STEPS = 8
    EARLY_LN = NB - BPB
    X_NORMALISED_AT = {0: 6, 1: 7}
    X_SPLIT_AT = {3: 2, 4: 3, 5: 4, 7: 5, 9: 6, 11: 7}
    HIGH_BY_DVE = (1, 7, 11, 15)

    early_at, early_width = columns_of(EARLY, NB)
    late_at, late_width = columns_of(LATE, NB)

    with ExitStack() as ctx:
        def sb(name, shape, dt=F32):
            return ctx.enter_context(nc.sbuf_tensor(name, shape, dt))

        def sb_over(name, shape, dt, base):
            return nc.alloc_sbuf_tensor_at(name, shape, dt, offset=base)

        def next_base():
            return -(-nc.sbuf_base // 32) * 32

        def sem(name):
            return ctx.enter_context(nc.semaphore(name))

        par = sb("par", [D, early_width])
        xrow = sb("xrow", [D, N])
        yH = sb("yH", [D, N], F32R)
        yL = sb("yL", [D, N], F32R)
        xT = sb("xT", [D, N])
        raw = sb("raw", [D, RING, HALF])
        split_base = next_base()
        aH = sb("aH", [D, 2, HALF], F32R)
        aL = sb("aL", [D, 2, HALF], F32R)
        kept = sb("kept", [D, 4, N])
        wH = sb("wH", [D, 2, D], F32R)
        wL = sb("wL", [D, 2, D], F32R)
        pt_base = next_base()
        ptH = sb("ptH", [D, 2, BANK], F32R)
        ptL = sb("ptL", [D, 2, BANK], F32R)
        oT = sb("oT", [D, 2 * D])
        lpar = sb_over("lpar", [D, late_width], F32, pt_base)
        scratch = sb_over("scratch", [D, 10, BANK], F32, split_base)
        s1 = sb("s1", [D, 2 * NB])
        s2 = sb("s2", [D, 2 * NB])
        s3 = sb("s3", [D, 2 * NB])
        mean = sb("mean", [D, NB])
        rstd = sb("rstd", [D, NB])
        shift = sb("shift", [D, NB])
        unorm = sb("unorm", [D, NB])
        epsu = sb("epsu", [D, NB])
        degp = sb("degp", [D, NB, 2])
        rdeg = sb("rdeg", [D, NB])
        cmax = sb("cmax", [D, 2, NCH])
        nmax = sb("nmax", [D, NB])
        psums = sb("psums", [D, NB, NCH])
        rsum = sb("rsum", [D, 2])
        umax = sb("umax", [D, 2])
        flag = sb("flag", [D, 1], I32)
        bsum = sb("bsum", [D, 2])
        ps = ctx.enter_context(nc.psum_tensor("ps", [D, 8, BANK], F32))

        def p(name, a=0, b=None):
            t, (at, w) = (par, early_at[name]) if name in EARLY else (lpar, late_at[name])
            return t[:, at + a:at + (w if b is None else b)]

        ident = p("ident")
        kept_tile = [kept[:, n // 2, (n % 2) * HALF:(n % 2 + 1) * HALF] for n in range(NKEPT)]
        rowbuf = raw[:, :, :].rearrange("p (s a) c -> p s (a c)", s=2)
        unitH = aH[:, :, :].rearrange("p a c -> p (a c)")
        unitL = aL[:, :, :].rearrange("p a c -> p (a c)")
        gT0, z0 = [[xT[:, i * BANK:(i + 1) * BANK] for i in slots] for slots in (range(BK - 2), range(BK - 2, BK))]
        msg_s, r_s, z_s, n_s, g_s = [[scratch[:, 2 * i + j, :] for j in range(2)] for i in range(5)]
        tmp = p("W2")
        stats = par[:, 0:NB * 6].rearrange("p (b s) -> p b s", s=6)
        assert NB * 6 <= early_at["W2"][0]
        uT = kept[0:NB, 2, 0:D]
        S_BANKS, PT_BANKS, O_BANK, OT_BANK = (0, 2), (4, 5), 6, 7
        S2 = [ps[:, s:s + 2, :].rearrange("p a c -> p (a c)") for s in S_BANKS]

        BY_ACT = [k for k in range(NBATCH) if k not in HIGH_BY_DVE]

        def chunk(t, c):
            return t[:, c * BANK:(c + 1) * BANK]

        par_landed = sem("par_landed")
        x_landed = [sem(f"x_landed{h}") for h in range(2)]
        late_landed = sem("late_landed")
        tile_landed = [sem(f"tile_landed{s}") for s in range(RING)]
        kept_landed = [sem(f"kept_landed{k}") for k in range(NKEPT)]
        aH_ready = sem("aH_ready")
        aL_ready = sem("aL_ready")
        tile_used = sem("tile_used")
        aH_used = sem("aH_used")
        w_ready = sem("w_ready")
        bank_done = sem("bank_done")
        g_ready = sem("g_ready")
        proj_done = sem("proj_done")
        z_ready = sem("z_ready")
        yH_ready = sem("yH_ready")
        yL_ready = sem("yL_ready")
        t_ready = sem("t_ready")
        dve_step = sem("dve_step")
        shift_ready = sem("shift_ready")
        act_norm_ready = sem("act_norm_ready")
        last_ready = sem("last_ready")
        scaled_ready = sem("scaled_ready")
        var_ready = sem("var_ready")
        root_ready = sem("root_ready")
        x_ready = sem("x_ready")
        stats_ready = sem("stats_ready")
        unit_ready = sem("unit_ready")
        unitT_done = sem("unitT_done")
        unitH_ready = sem("unitH_ready")
        unitL_ready = sem("unitL_ready")
        unorm_ready = sem("unorm_ready")
        unormT_done = sem("unormT_done")
        uT_ready = sem("uT_ready")
        u_written = sem("u_written")
        urow_landed = sem("urow_landed")
        umax_ready = sem("umax_ready")
        umax_all = sem("umax_all")
        row_landed = [sem(f"row_landed{r}") for r in range(2)]
        deg_done = sem("deg_done")
        bias_ready = sem("bias_ready")
        bw_step = sem("bw_step")
        bw_ready = sem("bw_ready")
        s_ready = sem("s_ready")
        m_ready = sem("m_ready")
        max_ready = sem("max_ready")
        exp_done = sem("exp_done")
        pt_ready = sem("pt_ready")
        ptH_ready = sem("ptH_ready")
        ptH_own = sem("ptH_own")
        ptL_ready = sem("ptL_ready")
        pv_done = sem("pv_done")
        o_copied = sem("o_copied")
        o_turned = sem("o_turned")
        o_step = sem("o_step")
        o_done = sem("o_done")
        xT_done = sem("xT_done")
        xT_ready = sem("xT_ready")
        self_done = sem("self_done")
        msg_done = sem("msg_done")
        msg_ready = sem("msg_ready")
        r_done = sem("r_done")
        zg_done = sem("zg_done")
        hn_done = sem("hn_done")
        in_done = sem("in_done")
        r_ready = sem("r_ready")
        zg_ready = sem("zg_ready")
        narg_ready = sem("narg_ready")
        n_ready = sem("n_ready")
        hn_used = sem("hn_used")
        gru_step = sem("gru_step")
        gru_ready = sem("gru_ready")
        self_ready = sem("self_ready")
        sum_ready = sem("sum_ready")
        gruT_done = sem("gruT_done")
        out_written = sem("out_written")
        waits_passed = sem("waits_passed")

        block = ctx.enter_context(nc.Block())

        def rounds(eng, n, peel):
            yield from range(peel)
            if n > peel:
                with eng.Fori(peel, n) as it:
                    yield it

        def wait_alone(eng, semaphore, value):
            eng.wait_ge(semaphore, value)
            if not isinstance(value, int):
                eng.sem_inc(waits_passed, 1)

        def wait_bank(eng, pass_index, b):
            h, j = divmod(b, HBK)
            if j == HBK - 1:
                eng.wait_ge(tile_used, (pass_index + 1) * TILES - 1 + h)
            else:
                eng.wait_ge(bank_done, pass_index * (BK - 2) + h * (HBK - 1) + j + 1)

        @block.sync
        def _(sp):
            adjT_tiles = adjT.rearrange("(b q) (h c) -> b h q c", q=D, h=2)
            adj_rows = adj.rearrange("(b q) c -> b q c", q=D)
            streamed = [(k, h) for k in range(SPAN) for h in range(2) if 2 * k + h not in KEPT_AT]

            def load_kept(which):
                for n in which:
                    it, i = divmod(n, len(KEPT_AT))
                    b, h = divmod(2 * SPAN * it + KEPT_AT[i], 2)
                    sp.dma_start(kept_tile[n], adjT_tiles[b, h]).then_inc(kept_landed[n], 16)

            def stream(ps_index):
                base = ps_index * TILES
                for it in rounds(sp, 2, 2 if ps_index in (0, 4) else 0):
                    for s, (k, h) in enumerate(streamed):
                        if ps_index == 4 and (it, s) == (0, RING):
                            sp.wait_ge(pv_done, NSB * NBATCH)
                            load_kept(range(NKEPT // 2, NKEPT))
                            sp.dma_start(lpar[:], late).then_inc(late_landed, 16)
                        if ps_index == 0 and (it, s) in kept_before:
                            load_kept([kept_before[it, s]])
                        if ps_index == 0 and (it, s) == (0, RING):
                            sp.dma_start(par[:], early).then_inc(par_landed, 16)
                        before = s - RING
                        k0, h0 = streamed[before]
                        count = 2 * k0 + h0 + 1 - (2 * SPAN if before < 0 else 0)
                        if not (ps_index == 0 and isinstance(it, int) and it == 0 and before < 0):
                            sp.wait_ge(aL_ready, it * (2 * SPAN) + (base + count))
                        sp.dma_start(raw[:, s % RING, :], adjT_tiles[it * SPAN + k, h]).then_inc(tile_landed[s % RING], 16)

            kept_before = {divmod(n * len(streamed) // len(KEPT_AT), len(streamed)): n for n in range(1, NKEPT)}
            for h in range(2):
                cols = slice(h * HALF, (h + 1) * HALF)
                sp.dma_start(xrow[:, cols], x_rows[:, cols]).then_inc(x_landed[h], 16)
                if h == 0:
                    load_kept([0])
            for q in range(4):
                stream(q)
            for r in range(2):
                sp.wait_ge(aL_ready, 4 * TILES - 2 + 2 * r)
                sp.dma_start(rowbuf[:, r, :], adj_rows[r]).then_inc(row_landed[r], 16)
            sp.wait_ge(uT_ready, 1)
            sp.dma_start(norms, uT).then_inc(u_written, 16)
            sp.wait_ge(u_written, 16)
            sp.dma_start(xT[:, 0:N], norms.rearrange("b d -> (b d)").partition_broadcast(D)).then_inc(urow_landed, 16)
            sp.wait_ge(urow_landed, 16)
            with sp.Fori(1, NSB) as sbi:
                for r in range(2):
                    sp.wait_ge(m_ready, sbi * (2 * NCH) + (r + 1 - 2) * NCH)
                    sp.dma_start(rowbuf[:, r, :], adj_rows[sbi * 2 + r]).then_inc(row_landed[r], 16)
            sp.wait_ge(m_ready, NB * NCH)
            sp.wait_ge(pt_ready, (NSB - 1) * NBATCH)
            load_kept(range(NKEPT // 2))
            stream(4)
            stream(5)
            out_blocks = out.rearrange("(b q) d -> q b d", q=D)
            by_dve = [c for c in range(BK) if c not in BY_ACT_LAST]
            for c in sorted(range(BK), key=lambda c: (by_dve if c in by_dve else BY_ACT_LAST).index(c)):
                if c in BY_ACT_LAST:
                    sp.wait_ge(last_ready, BY_ACT_LAST.index(c) + 1)
                else:
                    sp.wait_ge(x_ready, HBK + 2 * BK + by_dve.index(c) + 1)
                sp.dma_start(out_blocks[:, c * BPB:(c + 1) * BPB, :],
                             chunk(xrow, c).rearrange("p (b d) -> p b d", d=D)).then_inc(out_written, 16)
            sp.wait_ge(out_written, 16 * BK)

        @block.gpsimd
        def _(pool):
            def stage(pass_index, split, beside=None):
                for it in rounds(pool, BK, 1 if pass_index == 0 else 0):
                    wait_alone(pool, yL_ready, it + (split * BK + 1))
                    for r in range(BPB):
                        b = it * BPB + r
                        if not (pass_index == 0 and isinstance(it, int) and it == 0 and r < 2):
                            pool.wait_ge(tile_used, it * (2 * BPB) + (pass_index * TILES + 2 * r - 2))
                        pool.tensor_copy(wH[:, r % 2, :], yH[:, bass.ts(b, D)].bitcast(F32))
                        pool.tensor_copy(wL[:, r % 2, :], yL[:, bass.ts(b, D)].bitcast(F32)).then_inc(w_ready, 1)
                    if beside is not None:
                        beside(it)

            for q in range(4):
                stage(q, q)

            def stage_unit(rb, r, nth):
                if nth is not None:
                    pool.wait_ge(s_ready, nth)
                if not (isinstance(rb, int) and rb == 0):
                    wait_alone(pool, bw_ready, rb)
                c = bass.ts(rb, D)
                pool.tensor_tensor(tmp, unitH[:, c].bitcast(F32), unitL[:, c].bitcast(F32), ALU.add).then_inc(bw_step, 1)
                wait_alone(pool, bw_step, rb * 3 + 1)
                pool.tensor_scalar(tmp, tmp, p("beta"), 0.0, ALU.mult, ALU.add).then_inc(bw_step, 1)
                wait_alone(pool, bw_step, rb * 3 + 2)
                pool.tensor_copy(wH[:, r, :], tmp).then_inc(bw_step, 1)
                wait_alone(pool, bw_step, rb * 3 + 3)
                pool.tensor_tensor(wL[:, r, :], tmp, wH[:, r, :].bitcast(F32), ALU.subtract).then_inc(bw_ready, 1)

            def mask_bias(rb, r):
                for h in range(2):
                    wait_alone(pool, deg_done, rb * 2 + h + 1)
                    t = rowbuf[:, r, h * HALF:(h + 1) * HALF]
                    pool.tensor_scalar(t, t, -1.0, MASK, ALU.add, ALU.mult).then_inc(bias_ready, 1)

            mask_bias(0, 0)
            pool.wait_ge(umax_ready, 1)
            pool.partition_all_reduce(umax[:, 1:2], umax[:, 0:1], D, RMAX).then_inc(umax_all, 1)
            pool.wait_ge(tile_used, 4 * TILES)
            pool.wait_ge(unitL_ready, 1)
            for r in range(2):
                stage_unit(r, r, None)
            mask_bias(1, 1)
            pool.wait_ge(unitL_ready, BK)
            with pool.Fori(1, NSB) as sbi:
                for r in range(2):
                    stage_unit(sbi * 2 + r, r, sbi * (2 * NCH) + (r + 1 - 2) * NCH)
                    mask_bias(sbi * 2 + r, r)
            stage(4, 5)

            def residual(c):
                wait_alone(pool, self_ready, c + 1)
                t = xrow[:, bass.ts(c, BANK)]
                pool.tensor_tensor(t, t, xT[:, bass.ts(c, BANK)], ALU.add).then_inc(sum_ready, 1)

            stage(5, 6, beside=residual)

        @block.scalar
        def _(act):
            def split_high(pass_index, tiles=(0, TILES)):
                base = pass_index * TILES
                phase = pass_index if pass_index < 4 else pass_index - 4
                for it in rounds(act, 2, 2):
                    s = 0
                    for k in range(SPAN):
                        for h in range(2):
                            tile = 2 * SPAN * it + 2 * k + h
                            if not tiles[0] <= tile < tiles[1]:
                                s += 2 * k + h not in KEPT_AT
                                continue
                            if 2 * k + h in KEPT_AT:
                                n = len(KEPT_AT) * it + KEPT_AT.index(2 * k + h)
                                src = kept_tile[n]
                                if phase == 0:
                                    act.wait_ge(kept_landed[n], 16 * (1 if pass_index < 4 else 2))
                            else:
                                src = raw[:, s % RING, :]
                                uses = 2 * (2 * SPAN - len(KEPT_AT)) // RING
                                nth = pass_index * uses + it * (uses // 2) + s // RING + 1
                                act.wait_ge(tile_landed[s % RING], 16 * nth)
                                s += 1
                            if base + tile >= 2:
                                act.wait_ge(aH_used, base + tile - 1)
                                act.wait_ge(aL_ready, base + tile - 1)
                            nc.scalar.activation(aH[:, h, :], src, ACT.Copy).then_inc(aH_ready, 1)

            def high(c, src, split):
                nc.scalar.activation(chunk(yH, c), src, ACT.Copy).then_inc(yH_ready, 1)

            def project(tq, pass_index, func):
                for step in range(BK + (HBK if tq < 3 else 0)):
                    b = step
                    if b < BK:
                        wait_bank(act, pass_index, b)
                        if b >= len(gT0):
                            act.wait_ge(proj_done, tq * BK + b - len(gT0) + 1)
                        nc.scalar.activation(gT0[b % len(gT0)], ps[:, b, :], func).then_inc(g_ready, 1)
                    if b == HBK - 1 and tq < 3:
                        split_high(pass_index + 1, FIRST)
                    c = step - HBK
                    if c == HBK and tq < 3:
                        split_high(pass_index + 1, SECOND)
                    if c >= 0 and tq < 3:
                        if tq == 1:
                            act.wait_ge(proj_done, tq * BK + c + 1)
                            high(c, ps[:, c, :], tq + 1)
                        else:
                            zn = (tq // 2) * BK + c
                            act.wait_ge(z_ready, zn + 1)
                            high(c, z0[c % 2], tq + 1)

            def normalise(c, done):
                for b in range(c * BPB, (c + 1) * BPB):
                    t = xrow[:, b * D:(b + 1) * D]
                    ins = nc.scalar.activation(t, t, ACT.Identity, bias=shift[:, b:b + 1], scale=rstd[:, b:b + 1])
                ins.then_inc(done, 1)

            def root(n, lo=0, hi=NB):
                w = slice(0, 2 * NB) if n == 0 else slice(lo, hi)
                act.wait_ge(var_ready, n + 1)
                nc.scalar.activation(s2[:, w], s1[:, w], ACT.Sqrt).then_inc(root_ready, 1)

            for c in range(BK):
                if c == HBK:
                    split_high(0, FIRST)
                if c % HBK == 0:
                    act.wait_ge(x_landed[c // HBK], 16)
                high(c, chunk(xrow, c), 0)
            for q in range(3):
                split_high(q, (1 if q == 0 else 2, TILES))
                project(q, q, ACT.Relu if q == 1 else ACT.Copy)
            split_high(3, (2, TILES))
            project(3, 3, ACT.Copy)
            def degrees(rb, r, h, sbi):
                if h == 0:
                    act.wait_ge(row_landed[r], sbi * 16 + 16)
                t = rowbuf[:, r, h * HALF:(h + 1) * HALF]
                nc.scalar.activation(t, t, ACT.Copy, accum_out=degp[:, bass.ds(rb, 1), h]).then_inc(deg_done, 1)

            def exponent(rb, slot, c):
                if c == 0:
                    act.wait_ge(max_ready, rb + 1)
                t = kept[:, slot, c * CH:(c + 1) * CH]
                nc.scalar.activation(t, t, ACT.Exp, bias=nmax[:, bass.ds(rb, 1)],
                                     accum_out=psums[:, bass.ds(rb, 1), c]).then_inc(exp_done, 1)

            def turned_high(sbi, k):
                n = sbi * NBATCH + k
                act.wait_ge(pt_ready, n + 1)
                if not (isinstance(sbi, int) and sbi == 0 and k < 2):
                    act.wait_ge(pv_done, n - 1)
                nc.scalar.activation(ptH[:, k % 2, :], ps[:, PT_BANKS[k % 2], :], ACT.Copy).then_inc(ptH_ready, 1)

            def o_copy(sbi):
                act.wait_ge(pv_done, sbi * NBATCH + NBATCH)
                nc.scalar.activation(oT[:], ps[:, O_BANK, 0:2 * D], ACT.Copy).then_inc(o_copied, 1)

            def x_turned(ln, c):
                act.wait_ge(xT_done, (ln - 1) * BK + c + 1)
                nc.scalar.activation(chunk(xT, c), ps[:, c, :], ACT.Copy).then_inc(xT_ready, 1)

            def high_after(ln, c, split):
                act.wait_ge(x_ready, HBK + (ln - 1) * BK + c + 1)
                high(c, chunk(xrow, c), split)

            def super_block(sbi, parity, more, before):
                nxt = sbi + 1
                first_r0, first_r1 = 2 * NCH + 1 - LEAD, 4 * NCH + 1 - LEAD
                for k in range(NBATCH):
                    if k == 0 and before:
                        o_copy(sbi - 1)
                    if k not in HIGH_BY_DVE:
                        turned_high(sbi, k)
                    if k + NBATCH - first_r1 < NCH and before:
                        exponent(sbi * 2 + 1, 2 * parity + 1, k + NBATCH - first_r1)
                    if first_r0 <= k < first_r0 + NCH and more >= 1:
                        exponent(nxt * 2, 2 * (1 - parity), k - first_r0)
                    if k >= first_r1 and more >= 1:
                        exponent(nxt * 2 + 1, 2 * (1 - parity) + 1, k - first_r1)
                    if k in (1, 3) and more >= 1:
                        degrees(nxt * 2 + 1, 1, k // 2, nxt)
                    if k in (9, 11) and more == 2:
                        degrees((nxt + 1) * 2, 0, (k - 9) // 2, nxt + 1)
                    if more == 0 and k == 3:
                        root(1, 0, EARLY_LN)
                    if more == 0 and 0 <= k - SCALE_STEPS - 3 < HBK:
                        x_turned(1, k - SCALE_STEPS - 3)
                    if not before and 1 <= k < 3:
                        normalise_and_high(k + 1)
                    if not before and 3 <= k < 3 + HBK:
                        high_of_x(HBK + k - 3)

            for h in range(2):
                degrees(0, 0, h, 0)
            root(0)
            act.wait_ge(unormT_done, 1)
            nc.scalar.activation(uT, ps[0:NB, OT_BANK, 0:D], ACT.Copy).then_inc(uT_ready, 1)
            for c in range(BK):
                act.wait_ge(unitT_done, c + 1)
                nc.scalar.activation(chunk(unitH, c), ps[:, c, :], ACT.Copy).then_inc(unitH_ready, 1)
            for h in range(2):
                degrees(1, 1, h, 0)

            def high_of_x(c):
                act.wait_ge(x_ready, c - HBK + 1)
                high(c, chunk(xrow, c), 4)

            act.wait_ge(unit_ready, BK)
            act.wait_ge(shift_ready, 1)

            def normalise_and_high(c):
                normalise(c, act_norm_ready)
                act.wait_ge(act_norm_ready, c + 1)
                high(c, chunk(xrow, c), 4)

            for c in range(2):
                normalise_and_high(c)
            for r in range(2):
                for c in range(NCH):
                    exponent(r, r, c)
                    if r == 1 and c < 2:
                        degrees(2, 0, c, 1)
            super_block(0, 0, 2, False)
            with act.Fori(0, (NSB - 4) // 2) as it:
                super_block(it * 2 + 1, 1, 2, True)
                super_block(it * 2 + 2, 0, 2, True)
            super_block(NSB - 3, 1, 2, True)
            super_block(NSB - 2, 0, 1, True)
            super_block(NSB - 1, 1, 0, True)
            o_copy(NSB - 1)
            for c in range(HBK):
                high_after(1, c, 5)
            root(2, EARLY_LN, NB)
            split_high(4, FIRST)
            for c in range(HBK, BK - 1):
                high_after(1, c, 5)
            for c in range(HBK, BK - 1):
                x_turned(1, c)
            high_after(1, BK - 1, 5)
            x_turned(1, BK - 1)
            split_high(4, (1, TILES))
            for c in range(BK):
                wait_bank(act, 4, c)
                nc.scalar.activation(chunk(xrow, c), ps[:, c, :], ACT.Copy).then_inc(g_ready, 1)

            def message(c):
                act.wait_ge(msg_done, c + 1)
                nc.scalar.activation(msg_s[c % 2], ps[:, 0, :], ACT.Relu, bias=p("bm")).then_inc(msg_ready, 1)

            message(0)
            for c in range(BK):
                if c + 1 < BK:
                    message(c + 1)
                act.wait_ge(r_done, c + 1)
                nc.scalar.activation(r_s[c % 2], ps[:, 1, :], ACT.Sigmoid, bias=bsum[:, 0:1]).then_inc(r_ready, 1)
                act.wait_ge(zg_done, c + 1)
                nc.scalar.activation(z_s[c % 2], ps[:, 2, :], ACT.Sigmoid, bias=bsum[:, 1:2]).then_inc(zg_ready, 1)
                act.wait_ge(narg_ready, c + 1)
                nc.scalar.activation(n_s[c % 2], chunk(xrow, c), ACT.Tanh, bias=p("bih", 2, 3)).then_inc(n_ready, 1)
            root(3)

            for step in range(BK + 3):
                if step == BK:
                    split_high(5, FIRST)
                if step < BK:
                    high_after(2, step, 6)
                if 0 <= step - 1 < BK:
                    x_turned(2, step - 1)
                c = step - 3
                if c >= 0:
                    act.wait_ge(self_done, c + 1)
                    nc.scalar.activation(chunk(xT, c), ps[:, c, :], ACT.Copy).then_inc(self_ready, 1)
            split_high(5, (1, TILES))
            act.wait_ge(sum_ready, BK)
            for step in range(BK + HBK):
                if step < BK:
                    wait_bank(act, 5, step)
                    nc.scalar.activation(chunk(xT, step), ps[:, step, :], ACT.Copy).then_inc(g_ready, 1)
                c = step - HBK
                if c >= 0:
                    act.wait_ge(proj_done, 4 * BK + c + 1)
                    if c == 0:
                        act.wait_ge(tile_used, 6 * TILES)
                    for i in range(BPB):
                        b = c * BPB + i
                        ins = nc.scalar.activation(scratch[:, c, i * D:(i + 1) * D], ps[:, c, i * D:(i + 1) * D],
                                                   ACT.Copy, scale=rdeg[:, b:b + 1])
                    ins.then_inc(scaled_ready, 1)
            root(4)
            act.wait_ge(shift_ready, 2)
            for c in BY_ACT_LAST:
                normalise(c, last_ready)

        @block.vector
        def _(dve):
            chain = [0]

            def count(ins):
                chain[0] += 1
                ins.then_inc(dve_step, 1)

            def link(ins):
                count(ins)
                dve.wait_ge(dve_step, chain[0])

            def split_low(pass_index, tiles=(0, TILES)):
                base = pass_index * TILES
                for it in rounds(dve, 2, 2):
                    s = 0
                    for k in range(SPAN):
                        for h in range(2):
                            if 2 * k + h in KEPT_AT:
                                src = kept_tile[len(KEPT_AT) * it + KEPT_AT.index(2 * k + h)]
                            else:
                                src = raw[:, s % RING, :]
                                s += 1
                            tile = 2 * SPAN * it + 2 * k + h
                            if not tiles[0] <= tile < tiles[1]:
                                continue
                            if base + tile >= 2:
                                dve.wait_ge(tile_used, base + tile - 1)
                            dve.wait_ge(aH_ready, base + tile + 1)
                            dve.tensor_tensor(aL[:, h, :], src, aH[:, h, :].bitcast(F32), ALU.subtract).then_inc(aL_ready, 1)

            def low(c, src, split):
                dve.wait_ge(yH_ready, split * BK + c + 1)
                dve.tensor_tensor(chunk(yL, c), src, chunk(yH, c).bitcast(F32), ALU.subtract).then_inc(yL_ready, 1)

            def project(tq):
                split_low(tq + 1, FIRST)
                for step in range(BK + 1):
                    c = step
                    if c < BK and tq != 1:
                        zn = (tq // 2) * BK + c
                        dve.wait_ge(proj_done, tq * BK + c + 1)
                        if zn >= 2:
                            dve.wait_ge(yL_ready, (tq + 1) * BK + c - 1 if c >= 2 else tq * BK + BK)
                        filt = p("f1" if tq == 0 else "f2", c * BPB, (c + 1) * BPB)
                        dve.tensor_tensor(z0[c % 2].rearrange("p (b d) -> p b d", d=D),
                                          ps[:, c, :].rearrange("p (b d) -> p b d", d=D),
                                          filt.unsqueeze(2).to_broadcast([D, BPB, D]), ALU.mult).then_inc(z_ready, 1)
                    c = step - 1
                    if c >= 0:
                        if tq == 1:
                            low(c, ps[:, c, :], tq + 1)
                        else:
                            dve.wait_ge(z_ready, (tq // 2) * BK + c + 1)
                            low(c, z0[c % 2], tq + 1)

            def bank_stats(c, own, value):
                dve.wait_ge(own, value)
                for b in range(c * BPB, (c + 1) * BPB):
                    ins = dve.bn_stats(stats[:, b:b + 1, :], xrow[:, b * D:(b + 1) * D])
                ins.then_inc(stats_ready, 1)

            def scale_step(i, nroot, value, lo=0, hi=NB):
                raw_m2, m, d, v = s3[:, NB + lo:NB + hi], s3[:, lo:hi], s2[:, lo:hi], s1[:, lo:hi]
                norms_too = nroot == 0
                w = slice(0, 2 * NB) if norms_too else slice(lo, hi)
                a, r, q = s1[:, w], s2[:, w], s3[:, w]
                if i == 0:
                    dve.wait_ge(stats_ready, value)
                    dve.tensor_tensor(raw_m2, stats[:, lo:hi, 2], stats[:, lo:hi, 5], ALU.add)
                    dve.tensor_tensor(m, stats[:, lo:hi, 1], stats[:, lo:hi, 4], ALU.add)
                    count(dve.tensor_tensor(d, stats[:, lo:hi, 1], stats[:, lo:hi, 4], ALU.subtract))
                    return
                if i == 3:
                    dve.wait_ge(root_ready, nroot + 1)
                else:
                    dve.wait_ge(dve_step, chain[0])
                if i == 1:
                    dve.tensor_scalar(mean[:, lo:hi], m, 0.5, None, ALU.mult)
                    dve.tensor_scalar(v, raw_m2, 1.0 / D, LN_EPS, ALU.mult, ALU.add)
                    count(dve.scalar_tensor_tensor(out=d, in0=d, scalar=0.25, in1=d, op0=ALU.mult, op1=ALU.mult))
                elif i == 2 and norms_too:
                    link(dve.scalar_tensor_tensor(out=s1[:, NB:2 * NB], in0=d, scalar=float(D), in1=raw_m2, op0=ALU.mult, op1=ALU.add))
                    dve.tensor_scalar(s1[:, NB:2 * NB], s1[:, NB:2 * NB], TINY, None, ALU.max)
                    dve.tensor_tensor(v, v, d, ALU.add).then_inc(var_ready, 1)
                elif i == 2:
                    dve.tensor_tensor(v, v, d, ALU.add).then_inc(var_ready, 1)
                elif i == 3:
                    count(dve.reciprocal(q, r))
                elif i == 4:
                    count(dve.tensor_tensor(q, q, a, ALU.mult))
                elif i == 5:
                    count(dve.tensor_tensor(q, q, r, ALU.add))
                elif i == 6:
                    count(dve.tensor_scalar(r, q, 0.5, None, ALU.mult))
                elif i == 7 and norms_too:
                    link(dve.reciprocal(q, r))
                    link(dve.tensor_tensor(unorm[:], s2[:, 0:NB], s3[:, NB:2 * NB], ALU.mult))
                    dve.tensor_reduce(umax[:, 0:1], unorm[:], AX.X, ALU.max).then_inc(umax_ready, 1)
                    dve.tensor_scalar(epsu[:], unorm[:], COS_EPS, None, ALU.mult).then_inc(unorm_ready, 1)
                    link(dve.tensor_copy(rstd[:], s3[:, 0:NB]))
                elif i == 7:
                    link(dve.reciprocal(rstd[:, lo:hi], r))

            def row_scales(nroot, value):
                for i in range(SCALE_STEPS):
                    scale_step(i, nroot, value)

            def shift_of_rows():
                dve.scalar_tensor_tensor(out=shift[:], in0=mean[:], scalar=-1.0, in1=rstd[:], op0=ALU.mult,
                                         op1=ALU.mult).then_inc(shift_ready, 1)

            def normalise(c):
                for b in range(c * BPB, (c + 1) * BPB):
                    t = xrow[:, b * D:(b + 1) * D]
                    ins = dve.tensor_scalar(t, t, mean[:, b:b + 1], rstd[:, b:b + 1], ALU.subtract, ALU.mult)
                ins.then_inc(x_ready, 1)

            for c in range(BK):
                if c == HBK:
                    split_low(0, FIRST)
                low(c, chunk(xrow, c), 0)
            for q in range(3):
                split_low(q, (1, TILES))
                project(q)
            split_low(3, (1, TILES))
            for c in range(BK):
                dve.wait_ge(proj_done, 3 * BK + c + 1)
                dve.tensor_tensor(chunk(xrow, c), ps[:, c, :], chunk(xrow, c), ALU.add).then_inc(t_ready, 1)
                if c >= 1:
                    bank_stats(c - 1, t_ready, c)
            bank_stats(BK - 1, t_ready, BK)
            row_scales(0, BK)

            for step in range(BK + 2):
                if step < BK:
                    for b in range(step * BPB, (step + 1) * BPB):
                        ins = dve.tensor_scalar(kept[:, 3, b * D:(b + 1) * D], xrow[:, b * D:(b + 1) * D],
                                                mean[:, b:b + 1], s3[:, NB + b:NB + b + 1], ALU.subtract, ALU.mult)
                    ins.then_inc(unit_ready, 1)
                c = step - 2
                if c >= 0:
                    dve.wait_ge(unitH_ready, c + 1)
                    dve.tensor_tensor(chunk(unitL, c), ps[:, c, :], chunk(unitH, c).bitcast(F32), ALU.subtract).then_inc(unitL_ready, 1)
            shift_of_rows()
            dve.wait_ge(unit_ready, BK)
            dve.wait_ge(umax_all, 1)
            link(dve.tensor_scalar(flag[:], umax[:, 1:2], PRODUCT_SAFE, None, ALU.is_gt))
            small_norms = dve.value_load(flag[0:1, 0:1], min_val=0, max_val=1)

            def mask(rb, r, slot, c):
                n = rb * NCH + c
                with dve.If(small_norms > 0):
                    dve.wait_ge(s_ready, n + 1)
                    dve.wait_ge(urow_landed, 16)
                    corr = kept[:, slot, c * CH:(c + 1) * CH]
                    dve.tensor_scalar(corr, xT[:, c * CH:(c + 1) * CH], epsu[:, bass.ds(rb, 1)], 1.0, ALU.mult, ALU.add)
                    dve.drain()
                    dve.reciprocal(corr, corr)
                    dve.drain()
                    dve.tensor_tensor(S2[c % 2], S2[c % 2], corr, ALU.mult)
                    dve.drain()
                wait_alone(dve, s_ready, n + 1)
                if c in (0, NCH // 2):
                    wait_alone(dve, bias_ready, rb * 2 + c // (NCH // 2) + 1)
                dve.tensor_tensor_reduce(kept[:, slot, c * CH:(c + 1) * CH], S2[c % 2], rowbuf[:, r, c * CH:(c + 1) * CH],
                                         1.0, LOWEST, ALU.add, ALU.max, cmax[:, r, c:c + 1]).then_inc(m_ready, 1)
                if c == NCH - 1:
                    dve.wait_ge(m_ready, n + 1)
                    dve.tensor_reduce(nmax[:, bass.ds(rb, 1)], cmax[:, r, :], AX.X, ALU.max,
                                      negate=True).then_inc(max_ready, 1)

            def turned_low(sbi, k):
                if k in HIGH_BY_DVE:
                    own = HIGH_BY_DVE.index(k)
                    dve.wait_ge(pt_ready, sbi * NBATCH + k + 1)
                    if not (isinstance(sbi, int) and sbi == 0 and k < 2):
                        dve.wait_ge(pv_done, sbi * NBATCH + (k - 1))
                    dve.tensor_copy(ptH[:, k % 2, :], ps[:, PT_BANKS[k % 2], :]).then_inc(ptH_own, 1)
                    dve.wait_ge(ptH_own, sbi * len(HIGH_BY_DVE) + (own + 1))
                else:
                    dve.wait_ge(ptH_ready, sbi * len(BY_ACT) + (BY_ACT.index(k) + 1))
                dve.tensor_tensor(ptL[:, k % 2, :], ps[:, PT_BANKS[k % 2], :], ptH[:, k % 2, :].bitcast(F32),
                                  ALU.subtract).then_inc(ptL_ready, 1)

            def o_rows(sbi):
                rows = bass.ds(sbi * 2, 2)
                dve.wait_ge(o_turned, sbi + 1)
                dve.tensor_reduce(rsum[:], psums[:, rows, :], AX.X, ALU.add).then_inc(o_step, 1)
                dve.wait_ge(o_step, sbi * 2 + 1)
                dve.reciprocal(rsum[:], rsum[:]).then_inc(o_step, 1)
                dve.wait_ge(o_step, sbi * 2 + 2)
                for r in range(2):
                    b = sbi * 2 + r
                    t = xrow[:, bass.ts(b, D)]
                    ins = dve.scalar_tensor_tensor(out=t, in0=ps[:, OT_BANK, r * D:(r + 1) * D], scalar=rsum[:, r:r + 1],
                                                   in1=t, op0=ALU.mult, op1=ALU.add)
                ins.then_inc(o_done, 1)

            def o_stats(sbi):
                wait_alone(dve, o_done, sbi + 1)
                for r in range(2):
                    b = sbi * 2 + r
                    dve.bn_stats(stats[:, bass.ds(b, 1), :], xrow[:, bass.ts(b, D)]).then_inc(stats_ready, 1)

            def mask_chunk(sbi, parity, m):
                r, c = divmod(m, NCH)
                mask(sbi * 2 + r, r, 2 * parity + r, c)

            def super_block(sbi, parity, more, before):
                for k in range(NBATCH):
                    if not before and k in X_NORMALISED_AT:
                        normalise(X_NORMALISED_AT[k])
                    if not before and k in X_SPLIT_AT:
                        low(X_SPLIT_AT[k], chunk(xrow, X_SPLIT_AT[k]), 4)
                    m = (k + LEAD - 2) // 2
                    if k % 2 == 0 and m < 2 * NCH and more >= 1:
                        mask_chunk(sbi + 1, 1 - parity, m)
                    if k % 2 == 0 and m >= 2 * NCH and more == 2:
                        mask_chunk(sbi + 2, parity, m - 2 * NCH)
                    turned_low(sbi, k)
                    if k == 5 and before:
                        o_rows(sbi - 1)
                    if k == 9 and before:
                        o_stats(sbi - 1)
                    if more == 0 and k < SCALE_STEPS:
                        scale_step(k, 1, BK + EARLY_LN, 0, EARLY_LN)
                    if more == 0 and 0 <= k - SCALE_STEPS < BK - 1:
                        normalise(k - SCALE_STEPS)

            for m in range(2 * NCH):
                mask_chunk(0, 0, m)
            for c in range(2):
                low(c, chunk(xrow, c), 4)
                normalise(HBK + c)
            mask_chunk(1, 1, 0)
            super_block(0, 0, 2, False)
            with dve.Fori(0, (NSB - 4) // 2) as it:
                super_block(it * 2 + 1, 1, 2, True)
                super_block(it * 2 + 2, 0, 2, True)
            super_block(NSB - 3, 1, 2, True)
            super_block(NSB - 2, 0, 1, True)
            super_block(NSB - 1, 1, 0, True)
            o_rows(NSB - 1)
            o_stats(NSB - 1)
            for i in range(SCALE_STEPS):
                scale_step(i, 2, BK + NB, EARLY_LN, NB)
                if i < BK - 1:
                    low(i, chunk(xrow, i), 5)
            normalise(BK - 1)
            low(BK - 1, chunk(xrow, BK - 1), 5)

            def normalise_and_split(split):
                for step in range(BK + 1):
                    if step < BK:
                        normalise(step)
                    if step >= 1:
                        low(step - 1, chunk(xrow, step - 1), split)

            dve.tensor_tensor(bsum[:], p("bih", 0, 2), p("bhh", 0, 2), ALU.add)
            split_low(4)
            link(dve.tensor_reduce(rdeg[:], degp[:], AX.X, ALU.add))
            link(dve.tensor_scalar(rdeg[:], rdeg[:], 1.0, None, ALU.max))
            link(dve.reciprocal(rdeg[:], rdeg[:]))

            def gru_rows(c):
                dve.wait_ge(gruT_done, c + 1)
                dve.tensor_copy(chunk(xrow, c), ps[:, 5, :]).then_inc(t_ready, 1)

            for c in range(BK):
                h, t, ng, zg = chunk(xT, c), g_s[c % 2], n_s[c % 2], z_s[c % 2]
                narg = chunk(xrow, c)
                dve.wait_ge(r_ready, c + 1)
                dve.wait_ge(hn_done, c + 1)
                dve.scalar_tensor_tensor(out=narg, in0=ps[:, 4, :], scalar=p("bhh", 2, 3), in1=r_s[c % 2],
                                         op0=ALU.add, op1=ALU.mult).then_inc(hn_used, 1)
                dve.wait_ge(hn_used, c + 1)
                dve.wait_ge(in_done, c + 1)
                dve.tensor_tensor(narg, narg, ps[:, 3, :], ALU.add).then_inc(narg_ready, 1)
                if c >= 1:
                    gru_rows(c - 1)
                dve.wait_ge(n_ready, c + 1)
                dve.tensor_tensor(t, h, ng, ALU.subtract).then_inc(gru_step, 1)
                dve.wait_ge(gru_step, 3 * c + 1)
                dve.wait_ge(zg_ready, c + 1)
                dve.tensor_tensor(t, t, zg, ALU.mult).then_inc(gru_step, 1)
                dve.wait_ge(gru_step, 3 * c + 2)
                dve.tensor_tensor(t, t, ng, ALU.add).then_inc(gru_step, 1)
                dve.wait_ge(gru_step, 3 * c + 3)
                dve.tensor_tensor(t, t, h, ALU.add).then_inc(gru_ready, 1)
                if c >= 1:
                    bank_stats(c - 1, t_ready, BK + c)
            gru_rows(BK - 1)
            bank_stats(BK - 1, t_ready, 2 * BK)
            row_scales(3, 2 * BK + NB)

            normalise_and_split(6)
            split_low(5)
            dve.wait_ge(sum_ready, BK)
            for c in range(BK):
                dve.wait_ge(scaled_ready, c + 1)
                dve.tensor_tensor(chunk(xrow, c), scratch[:, c, :], chunk(xrow, c), ALU.add).then_inc(t_ready, 1)
                if c >= 1:
                    bank_stats(c - 1, t_ready, 2 * BK + c)
            bank_stats(BK - 1, t_ready, 3 * BK)
            row_scales(4, 3 * BK + NB)
            shift_of_rows()
            for c in range(BK):
                if c not in BY_ACT_LAST:
                    normalise(c)

        @block.tensor
        def _(pe):
            def multiply(pass_index, read=None, value=0):
                def tiles(it, first, last):
                    for r in range(2):
                        for h in range(2):
                            tile = 4 * it + (pass_index * TILES + 2 * r + h)
                            banks = [ps[:, h * HBK + j, :] for j in range(HBK)]
                            cols = [slice(j * BANK, (j + 1) * BANK) for j in range(HBK)]
                            if h == 0:
                                pe.wait_ge(w_ready, 2 * it + (pass_index * NB + r + 1))
                            if first and r == 0 and read is not None:
                                pe.wait_ge(read, value - (HBK if h == 0 else 0))
                            pe.wait_ge(aH_ready, tile + 1)
                            for b, c in zip(banks, cols):
                                pe.matmul(b, wH[:, r, :], aH[:, h, c], start=first and r == 0, stop=False)
                            for b, c in zip(banks, cols):
                                ins = pe.matmul(b, wL[:, r, :], aH[:, h, c], start=False, stop=False)
                            ins.then_inc(aH_used, 1)
                            pe.wait_ge(aL_ready, tile + 1)
                            done = last and r == 1
                            for b, c in zip(banks, cols):
                                ins = pe.matmul(b, wH[:, r, :], aL[:, h, c], start=False, stop=done)
                                if done and c.stop < HALF:
                                    ins.then_inc(bank_done, 1)
                            ins.then_inc(tile_used, 1)
                tiles(0, True, False)
                with pe.Fori(1, NB // 2 - 1) as it:
                    tiles(it, False, False)
                tiles(NB // 2 - 1, False, True)

            def project(tq, weights, turned):
                for b in range(BK):
                    pe.wait_ge(g_ready, (tq if tq < 4 else 5) * BK + b + 1)
                    for i in range(BPB):
                        o, t = ps[:, b, i * D:(i + 1) * D], turned[b % len(turned)][:, i * D:(i + 1) * D]
                        if weights is None:
                            ins = pe.transpose(o, t, ident)
                        else:
                            ins = pe.matmul(o, t, weights, start=True, stop=True)
                    ins.then_inc(proj_done, 1)

            def turn_chunk(src, c, ready, base, done):
                pe.wait_ge(ready, base + c + 1)
                for i in range(BPB):
                    ins = pe.transpose(ps[:, c, i * D:(i + 1) * D], src[:, c * BANK + i * D:c * BANK + (i + 1) * D], ident)
                ins.then_inc(done, 1)

            for q in range(4):
                multiply(q, *[(), (z_ready, BK), (yL_ready, 3 * BK), (z_ready, 2 * BK)][q])
                if q == 0:
                    pe.wait_ge(par_landed, 16)
                project(q, [p("W1"), p("W2"), None, None][q], gT0)

            pe.wait_ge(unorm_ready, 1)
            pe.transpose(ps[0:NB, OT_BANK, 0:D], unorm[:], ident).then_inc(unormT_done, 1)
            for c in range(BK):
                if c == OT_BANK:
                    pe.wait_ge(uT_ready, 1)
                turn_chunk(kept[:, 3, :], c, unit_ready, 0, unitT_done)

            def scores(sbi, q):
                m, j = divmod(q, CH // BANK)
                r, c = divmod(m, NCH)
                if j == 0:
                    if c == 0:
                        pe.wait_ge(bw_ready, sbi * 2 + (r + 1))
                    if not (isinstance(sbi, int) and sbi == 0 and m < 2):
                        pe.wait_ge(m_ready, sbi * (2 * NCH) + (m - 1))
                o = ps[:, S_BANKS[c % 2] + j, :]
                col = slice(c * CH + j * BANK, c * CH + (j + 1) * BANK)
                pe.matmul(o, wH[:, r, :], unitH[:, col], start=True, stop=False)
                pe.matmul(o, wH[:, r, :], unitL[:, col], start=False, stop=False)
                ins = pe.matmul(o, wL[:, r, :], unitH[:, col], start=False, stop=True)
                if j == CH // BANK - 1:
                    ins.then_inc(s_ready, 1)

            def turn_batch(sbi, parity, k, first):
                n = sbi * NBATCH + k
                if k % (NBATCH // NCH) == 0:
                    pe.wait_ge(exp_done, sbi * (2 * NCH) + (NCH + k // (NBATCH // NCH) + 1))
                if not first:
                    pe.wait_ge(ptL_ready, n - 1)
                for a in range(2):
                    for r in range(2):
                        j = 2 * k + a
                        ins = pe.transpose(ps[:, PT_BANKS[k % 2], (2 * a + r) * D:(2 * a + r + 1) * D],
                                           kept[:, 2 * parity + r, j * D:(j + 1) * D], ident)
                ins.then_inc(pt_ready, 1)

            def sum_batch(sbi, k, before):
                n = sbi * NBATCH + k
                if k == 0 and before:
                    pe.wait_ge(o_copied, sbi)
                pe.wait_ge(ptL_ready, n + 1)
                if not before and k % 2 == 0:
                    pe.wait_ge(yL_ready, 4 * BK + k // 2 + 1)
                o = ps[:, O_BANK, 0:2 * D]
                for a in range(2):
                    j = 2 * k + a
                    jc, cols = slice(j * D, (j + 1) * D), slice(a * 2 * D, (a + 1) * 2 * D)
                    pe.matmul(o, yH[:, jc], ptH[:, k % 2, cols], start=(j == 0), stop=False)
                    pe.matmul(o, yH[:, jc], ptL[:, k % 2, cols], start=False, stop=False)
                    ins = pe.matmul(o, yL[:, jc], ptH[:, k % 2, cols], start=False, stop=(j == NB - 1))
                ins.then_inc(pv_done, 1)

            def turn_sums(sbi, first):
                pe.wait_ge(o_copied, sbi + 1)
                if not first:
                    pe.wait_ge(o_done, sbi)
                for r in range(2):
                    ins = pe.transpose(ps[:, OT_BANK, r * D:(r + 1) * D], oT[:, r * D:(r + 1) * D], ident)
                ins.then_inc(o_turned, 1)

            def super_block(sbi, parity, more, before, second=False):
                for k in range(NBATCH):
                    turn_batch(sbi, parity, k, not before and k < 2)
                    if k < NBATCH - LEAD and more >= 1:
                        scores(sbi + 1, k + LEAD)
                    if k >= NBATCH - LEAD and more == 2:
                        scores(sbi + 2, k - NBATCH + LEAD)
                    if k >= 1:
                        sum_batch(sbi, k - 1, before)
                    if k == 2 and before:
                        turn_sums(sbi - 1, second)
                    if more == 0 and 0 <= k - SCALE_STEPS - 2 < HBK:
                        turn_chunk(xrow, k - SCALE_STEPS - 2, x_ready, HBK, xT_done)
                sum_batch(sbi, NBATCH - 1, before)

            for q in range(NBATCH):
                if q < BK:
                    pe.wait_ge(unitL_ready, q + 1)
                scores(0, q)
            for q in range(LEAD):
                scores(1, q)
            super_block(0, 0, 2, False)
            super_block(1, 1, 2, True, True)
            super_block(2, 0, 2, True)
            with pe.Fori(1, (NSB - 4) // 2) as it:
                super_block(it * 2 + 1, 1, 2, True)
                super_block(it * 2 + 2, 0, 2, True)
            super_block(NSB - 3, 1, 2, True)
            super_block(NSB - 2, 0, 1, True)
            super_block(NSB - 1, 1, 0, True)
            turn_sums(NSB - 1, False)

            for c in range(HBK, BK):
                if c == BK - 1:
                    pe.wait_ge(o_done, NSB)
                turn_chunk(xrow, c, x_ready, HBK, xT_done)
            multiply(4, xT_ready, BK)
            pe.wait_ge(late_landed, 16)
            pe.wait_ge(g_ready, 5 * BK)

            def message(c):
                if c >= 1:
                    pe.wait_ge(msg_ready, c)
                pe.matmul(ps[:, 0, :], p("WmT"), chunk(xrow, c), start=True, stop=True).then_inc(msg_done, 1)

            def gru_turn(c):
                pe.wait_ge(gru_ready, c + 1)
                if c >= 1:
                    pe.wait_ge(t_ready, BK + c)
                for i in range(BPB):
                    ins = pe.transpose(ps[:, 5, i * D:(i + 1) * D], g_s[c % 2][:, i * D:(i + 1) * D], ident)
                ins.then_inc(gruT_done, 1)

            def gate(bank, wi, wh, c):
                pe.matmul(ps[:, bank, :], p("WhhT")[:, wh], chunk(xT, c), start=True, stop=False)
                return pe.matmul(ps[:, bank, :], p("WihT")[:, wi], msg_s[c % 2], start=False, stop=True)

            R, Z, NG = (slice(i * D, (i + 1) * D) for i in range(3))
            message(0)
            for c in range(BK):
                if c + 1 < BK:
                    message(c + 1)
                pe.wait_ge(msg_ready, c + 1)
                if c >= 1:
                    pe.wait_ge(r_ready, c)
                gate(1, R, R, c).then_inc(r_done, 1)
                if c >= 1:
                    pe.wait_ge(zg_ready, c)
                gate(2, Z, Z, c).then_inc(zg_done, 1)
                if c >= 1:
                    pe.wait_ge(hn_used, c)
                pe.matmul(ps[:, 4, :], p("WhhT")[:, NG], chunk(xT, c), start=True, stop=True).then_inc(hn_done, 1)
                if c >= 1:
                    pe.wait_ge(narg_ready, c)
                pe.matmul(ps[:, 3, :], p("WihT")[:, NG], msg_s[c % 2], start=True, stop=True).then_inc(in_done, 1)
                if c >= 1:
                    gru_turn(c - 1)
            gru_turn(BK - 1)

            for step in range(BK + 2):
                if step < BK:
                    turn_chunk(xrow, step, x_ready, HBK + BK, xT_done)
                c = step - 2
                if c >= 0:
                    pe.wait_ge(xT_ready, BK + c + 1)
                    for i in range(BPB):
                        ins = pe.matmul(ps[:, c, i * D:(i + 1) * D], chunk(xT, c)[:, i * D:(i + 1) * D], p("Ws"), start=True, stop=True)
                    ins.then_inc(self_done, 1)
            multiply(5, self_ready, BK)
            project(4, p("Wn"), [chunk(xT, b) for b in range(BK)])


NAMES = ("x_rows", "adjT", "adj", "early", "late")


def kernel(x, adj, L0_gnn_W1, L0_gnn_f1, L0_gnn_W2, L0_gnn_f2, L1_gnn_beta, L2_gnn_W_msg, L2_gnn_b_msg, L2_gnn_W_ih,
           L2_gnn_W_hh, L2_gnn_b_ih, L2_gnn_b_hh, L3_gnn_W_self, L3_gnn_W_neigh):
    import numpy as np
    import concourse.bacc as bacc
    from concourse.bass_utils import run_bass_kernel_spmd

    x, adj = np.asarray(x), np.asarray(adj)
    N = x.shape[0]
    NB = N // D

    def columns(v, n):
        return np.asarray(v).reshape(n, D).T

    packed = {
        "f1": columns(L0_gnn_f1, NB), "f2": columns(L0_gnn_f2, NB),
        "W1": np.asarray(L0_gnn_W1), "W2": np.asarray(L0_gnn_W2), "WmT": np.asarray(L2_gnn_W_msg).T,
        "WihT": np.asarray(L2_gnn_W_ih).T, "WhhT": np.asarray(L2_gnn_W_hh).T,
        "Ws": np.asarray(L3_gnn_W_self), "Wn": np.asarray(L3_gnn_W_neigh), "ident": np.eye(D, dtype=np.float32),
        "bm": columns(L2_gnn_b_msg, 1), "bih": columns(L2_gnn_b_ih, 3), "bhh": columns(L2_gnn_b_hh, 3),
        "beta": np.broadcast_to(np.asarray(L1_gnn_beta).reshape(1, 1), (D, 1)),
    }
    early, late = (np.ascontiguousarray(np.concatenate([packed[name] for name in names], axis=1)) for names in (EARLY, LATE))
    x_rows = np.ascontiguousarray(x.reshape(NB, D, D).transpose(1, 0, 2).reshape(D, N))
    arrays = {"x_rows": x_rows, "adjT": np.ascontiguousarray(adj.T), "adj": np.ascontiguousarray(adj), "early": early, "late": late}

    nc = bacc.Bacc("TRN2", target_bir_lowering=False, num_devices=1)
    args = [nc.dram_tensor(n, arrays[n].shape, F32, kind="ExternalInput").ap() for n in NAMES]
    out = nc.dram_tensor("out", (N, D), F32, kind="ExternalOutput").ap()
    norms = nc.dram_tensor("norms", (N // D, D), F32, kind="Internal").ap()
    build(nc, *args, norms, out)
    r = run_bass_kernel_spmd(nc, [arrays], core_ids=[0])
    return r.results[0]["out"]
```
